# Optimizing a Trainium2 kernel written in Bass

```python
import numpy as np
import jax
import jax.numpy as jnp

def _softmax(x, axis=-1):
    return jax.nn.softmax(x, axis=axis)

def _gelu(x):
    return jax.nn.gelu(x, approximate=True)

def _silu(x):
    return jax.nn.silu(x)

def _sigmoid(x):
    return jax.nn.sigmoid(x)

def _layernorm(x, axis=-1, eps=1e-05):
    m = jnp.mean(x, axis=axis, keepdims=True)
    v = jnp.var(x, axis=axis, keepdims=True)
    return (x - m) / jnp.sqrt(v + eps)

def _scatter_add(tgt, idx, src, axis=0):
    return tgt.at[idx].add(src)

def _segment_sum(src, seg, n):
    return jax.ops.segment_sum(src, seg, n)
kernel_name = 'mk_vit_tower_postln_d1_tok_img768_r4_71e3e2'

def setup_inputs(seed: int=0):
    np.random.seed(seed)
    _w = jnp.asarray

    def _rec_inputs():
        import jax
        import jax.numpy as jnp
        _rk = jax.random.key(seed)
        x = -0.00016672 + 0.999947 * jax.random.normal(jax.random.fold_in(_rk, 1), (16, 3, 96, 96), jnp.float32)
        return x
    x = _rec_inputs()

    def _L0_tok_setup():
        import jax, jax.numpy as jnp
        import numpy as np
        C, H, W = (3, 96, 96)
        PH, PW = (16, 16)
        EMBED = 192
        PATCH_DIM = C * PH * PW
        key = jax.random.key(seed)
        kx, kw, kb = jax.random.split(key, 3)
        x = jax.random.normal(kx, (64, C, H, W), dtype=jnp.float32)
        bound = 1.0 / np.sqrt(PATCH_DIM)
        Wp = jax.random.uniform(kw, (EMBED, PATCH_DIM), minval=-bound, maxval=bound, dtype=jnp.float32)
        bp = jax.random.uniform(kb, (EMBED,), minval=-bound, maxval=bound, dtype=jnp.float32)
        return {'x': x, 'Wp': Wp, 'bp': bp}
    _L0_tok_all = _L0_tok_setup()
    _L0_tok_in = {k: v for k, v in _L0_tok_all.items() if k in ('Wp', 'bp')}
    del _L0_tok_all

    def _L0_attn_setup():
        import jax, jax.numpy as jnp
        import numpy as np
        HEADS = 12
        HEAD_DIM = 64
        WINDOW = 65
        EMBED = 192
        B, L = (1, 512)
        key = jax.random.key(seed)
        k1, k2, k3 = jax.random.split(key, 3)
        x = jax.random.normal(k1, (B, L, EMBED), dtype=jnp.float32)
        w_qkv = jax.random.normal(k2, (EMBED, 3 * HEADS * HEAD_DIM), dtype=jnp.float32) * 0.02
        w_out = jax.random.normal(k3, (HEADS * HEAD_DIM, EMBED), dtype=jnp.float32) * 0.02
        b_out = jnp.zeros((EMBED,), dtype=jnp.float32)
        return {'x': x, 'w_qkv': w_qkv, 'w_out': w_out, 'b_out': b_out}
    _L0_attn_all = _L0_attn_setup()
    _L0_attn_in = {k: v for k, v in _L0_attn_all.items() if k in ('w_qkv', 'w_out', 'b_out')}
    del _L0_attn_all

    def _L0_ffn_setup():
        import jax, jax.numpy as jnp
        import numpy as np
        import math
        B, T, C = (8, 512, 192)
        E = 3
        HD = C // E
        TOPK = 2
        NGLOB = 4

        def _masked_softmax(att, mask):
            att = jnp.where(mask, -jnp.inf, att)
            return jax.nn.softmax(att, axis=-1)
        key = jax.random.key(seed)
        ks = jax.random.split(key, 16)
        s = 0.02
        return {'x': jax.random.normal(ks[0], (B, T, C), jnp.float32), 'Wqk': jax.random.normal(ks[1], (C, 2 * C), jnp.float32) * s, 'bqk': jnp.zeros((2 * C,), jnp.float32), 'Wv': jax.random.normal(ks[2], (E, C, HD), jnp.float32) * s, 'bv': jnp.zeros((E, HD), jnp.float32), 'conv_w': jax.random.normal(ks[3], (HD, 1, 3), jnp.float32) * s, 'conv_b': jnp.zeros((HD,), jnp.float32), 'glob': jax.random.normal(ks[4], (NGLOB, HD), jnp.float32) * 0.02, 'pos_bias': jnp.zeros((64, 64), jnp.float32), 'Wg1': jax.random.normal(ks[5], (C, 32), jnp.float32) * s, 'bg1': jnp.zeros((32,), jnp.float32), 'Wg2': jax.random.normal(ks[6], (32, E), jnp.float32) * s, 'bg2': jnp.zeros((E,), jnp.float32), 'Wp': jax.random.normal(ks[7], (C, C), jnp.float32) * s, 'bp': jnp.zeros((C,), jnp.float32)}
    _L0_ffn_all = _L0_ffn_setup()
    _L0_ffn_in = {k: v for k, v in _L0_ffn_all.items() if k in ('Wqk', 'bqk', 'Wv', 'bv', 'conv_w', 'conv_b', 'glob', 'pos_bias', 'Wg1', 'bg1', 'Wg2', 'bg2', 'Wp', 'bp')}
    del _L0_ffn_all
    return {'x': x, 'L0_tok_Wp': _L0_tok_in['Wp'], 'L0_tok_bp': _L0_tok_in['bp'], 'L0_attn_w_qkv': _L0_attn_in['w_qkv'], 'L0_attn_w_out': _L0_attn_in['w_out'], 'L0_attn_b_out': _L0_attn_in['b_out'], 'L0_ffn_Wqk': _L0_ffn_in['Wqk'], 'L0_ffn_bqk': _L0_ffn_in['bqk'], 'L0_ffn_Wv': _L0_ffn_in['Wv'], 'L0_ffn_bv': _L0_ffn_in['bv'], 'L0_ffn_conv_w': _L0_ffn_in['conv_w'], 'L0_ffn_conv_b': _L0_ffn_in['conv_b'], 'L0_ffn_glob': _L0_ffn_in['glob'], 'L0_ffn_pos_bias': _L0_ffn_in['pos_bias'], 'L0_ffn_Wg1': _L0_ffn_in['Wg1'], 'L0_ffn_bg1': _L0_ffn_in['bg1'], 'L0_ffn_Wg2': _L0_ffn_in['Wg2'], 'L0_ffn_bg2': _L0_ffn_in['bg2'], 'L0_ffn_Wp': _L0_ffn_in['Wp'], 'L0_ffn_bp': _L0_ffn_in['bp']}

def reference(x, L0_tok_Wp, L0_tok_bp, L0_attn_w_qkv, L0_attn_w_out, L0_attn_b_out, L0_ffn_Wqk, L0_ffn_bqk, L0_ffn_Wv, L0_ffn_bv, L0_ffn_conv_w, L0_ffn_conv_b, L0_ffn_glob, L0_ffn_pos_bias, L0_ffn_Wg1, L0_ffn_bg1, L0_ffn_Wg2, L0_ffn_bg2, L0_ffn_Wp, L0_ffn_bp):
    import jax
    import jax.numpy as jnp

    def _L0_tok_ref(x, Wp, bp):
        import jax, jax.numpy as jnp
        import numpy as np
        C, H, W = (3, 96, 96)
        PH, PW = (16, 16)
        EMBED = 192
        PATCH_DIM = C * PH * PW
        b, c, h, w = x.shape
        nph, npw = (h // PH, w // PW)
        p = x.reshape(b, c, nph, PH, npw, PW)
        p = p.transpose(0, 2, 4, 1, 3, 5).reshape(b, nph * npw, c * PH * PW)
        return jnp.einsum('bnd,ed->bne', p, Wp) + bp

    def _L0_attn_ref(x, w_qkv, w_out, b_out):
        import jax, jax.numpy as jnp
        import numpy as np
        HEADS = 12
        HEAD_DIM = 64
        WINDOW = 65
        EMBED = 192
        B, L = (1, 512)
        b, l, _ = x.shape
        pad = WINDOW // 2
        qkv = jnp.einsum('ble,ef->blf', x, w_qkv).reshape(b, l, HEADS, 3 * HEAD_DIM)
        q = qkv[..., :HEAD_DIM]
        k = qkv[..., HEAD_DIM:2 * HEAD_DIM]
        v = qkv[..., 2 * HEAD_DIM:]
        k_pad = jnp.pad(k, ((0, 0), (pad, pad), (0, 0), (0, 0)))
        v_pad = jnp.pad(v, ((0, 0), (pad, pad), (0, 0), (0, 0)))
        idx = jnp.arange(l)[:, None] + jnp.arange(WINDOW)[None, :]
        k_win = k_pad[:, idx]
        v_win = v_pad[:, idx]
        score = jnp.einsum('blhd,blwhd->blhw', q, k_win) / jnp.sqrt(jnp.asarray(HEAD_DIM, dtype=x.dtype))
        weights = jax.nn.softmax(score, axis=-1)
        out = jnp.einsum('blhw,blwhd->blhd', weights, v_win)
        out = out.reshape(b, l, HEADS * HEAD_DIM)
        return jnp.einsum('blf,fe->ble', out, w_out) + b_out

    def _L0_ffn_ref(x, Wqk, bqk, Wv, bv, conv_w, conv_b, glob, pos_bias, Wg1, bg1, Wg2, bg2, Wp, bp):
        import jax, jax.numpy as jnp
        import numpy as np
        import math
        B, T, C = (8, 512, 192)
        E = 3
        HD = C // E
        TOPK = 2
        NGLOB = 4

        def _masked_softmax(att, mask):
            att = jnp.where(mask, -jnp.inf, att)
            return jax.nn.softmax(att, axis=-1)
        Bx, Tx, Cx = x.shape
        scale = 1.0 / math.sqrt(HD)
        gate = jax.nn.softmax(jax.nn.relu(x @ Wg1 + bg1) @ Wg2 + bg2, axis=-1)
        top_w, top_i = jax.lax.top_k(gate, TOPK)
        top_w = jax.nn.softmax(top_w, axis=-1)
        qk = x @ Wqk + bqk
        q, k = (qk[..., :Cx], qk[..., Cx:])
        q = q.reshape(Bx, Tx, E, HD)
        k = k.reshape(Bx, Tx, E, HD)
        rows = jnp.arange(Tx)[:, None]
        ys = []
        for e in range(E):
            qe = q[:, :, e]
            ke = k[:, :, e]
            ve = x @ Wv[e] + bv[e]
            if e == 0:
                qc = jnp.transpose(qe, (0, 2, 1))
                qc = jax.lax.conv_general_dilated(qc, conv_w, window_strides=(1,), padding=((1, 1),), feature_group_count=HD, dimension_numbers=('NCH', 'OIH', 'NCH'))
                qe = jnp.transpose(qc + conv_b[None, :, None], (0, 2, 1))
            elif e == 1:
                gb = jnp.broadcast_to(glob[None], (Bx, NGLOB, HD))
                ke = jnp.concatenate([ke, gb], axis=1)
                ve = jnp.concatenate([ve, gb], axis=1)
            att = jnp.einsum('btd,bsd->bts', qe, ke) * scale
            if e == 2 and Tx <= 64:
                att = att + pos_bias[:Tx, :Tx][None]
            S = att.shape[-1]
            mask = jnp.arange(S)[None, :] > rows
            att = _masked_softmax(att, mask[None])
            ys.append(jnp.einsum('bts,bsd->btd', att, ve))
        ys = jnp.stack(ys, axis=2)
        w_e = jnp.sum(jax.nn.one_hot(top_i, E, dtype=x.dtype) * top_w[..., None], axis=-2)
        combined = (ys * w_e[..., None]).reshape(Bx, Tx, Cx)
        return combined @ Wp + bp
    h = _L0_tok_ref(x, L0_tok_Wp, L0_tok_bp)
    h = _layernorm(h + _L0_attn_ref(h, L0_attn_w_qkv, L0_attn_w_out, L0_attn_b_out), axis=-1)
    h = _layernorm(h + _L0_ffn_ref(h, L0_ffn_Wqk, L0_ffn_bqk, L0_ffn_Wv, L0_ffn_bv, L0_ffn_conv_w, L0_ffn_conv_b, L0_ffn_glob, L0_ffn_pos_bias, L0_ffn_Wg1, L0_ffn_bg1, L0_ffn_Wg2, L0_ffn_bg2, L0_ffn_Wp, L0_ffn_bp), axis=-1)
    return h

_drawn_inputs = setup_inputs


def setup_inputs(seed=0):
    import zlib

    import numpy as np

    out = dict(_drawn_inputs(seed))
    spreads = {'L0_attn_b_out': (0.0, 0.1),
     'L0_ffn_bqk': (0.0, 0.8),
     'L0_ffn_bv': (0.0, 0.694),
     'L0_ffn_conv_b': (0.0, 0.8),
     'L0_ffn_pos_bias': (0.0, 0.8),
     'L0_ffn_bg1': (0.0, 0.8),
     'L0_ffn_bg2': (0.0, 0.515),
     'L0_ffn_bp': (0.0, 0.1)}
    factors = {'L0_attn_w_qkv': 3.849,
     'L0_attn_w_out': 3.87,
     'L0_ffn_Wqk': 8.0,
     'L0_ffn_Wv': 4.834,
     'L0_ffn_conv_w': 8.0,
     'L0_ffn_Wg1': 8.0,
     'L0_ffn_Wg2': 8.0,
     'L0_ffn_Wp': 3.544}
    for name, (base, spread) in spreads.items():
        noise = np.random.default_rng([zlib.crc32(name.encode()), seed]).standard_normal(out[name].shape)
        drawn = base * np.exp(spread * noise) if base else spread * noise
        out[name] = jnp.asarray(drawn.astype(out[name].dtype))
    for name, factor in factors.items():
        out[name] = (out[name] * factor).astype(out[name].dtype)
    return out
```

```python
from contextlib import ExitStack

import concourse.bass as bass
from concourse import mybir

F32 = mybir.dt.float32
F32R = mybir.dt.float32r
BF16 = mybir.dt.bfloat16
ALU = mybir.AluOpType
ACT = mybir.ActivationFunctionType
AX = mybir.AxisListType

IMAGES, TOK, SLOT = 16, 36, 64
GROUPS, GI = 2, 8
GT = GI * TOK
TILES = GI // 2
DIM, CH, NCH = 192, 96, 2
PATCH, PK = 768, 6
PAIRS, HD = 6, 64
SCALE = 0.125
WINDOW_SIDE = 32
NEG = -1.0e30

C_IDENT, C_CAUSAL, C_OUTSIDE, C_EPS, C_MEAN = 0, 128, 164, 165, 166
C_END = C_MEAN + CH
B_TOK, B_OUT, B_FFN, B_QK, B_CONVW, B_CONVB, B_G1 = 0, 2, 4, 6, 10, 13, 14
B_END = 15

ATTN = [("attn", g, p) for g in range(GROUPS) for p in range(PAIRS)]
LINE = ATTN + [("ffn", 0, 0), ("ffn", 0, 1), None, None, None, ("ffn", 1, 0), ("ffn", 1, 1)]
QK_RING = 3
STEPS = {
    0: [("v", 0, 0), ("v", 0, 1)], 1: [("v", 0, 2), ("v", 0, 3)],
    4: [("v", 1, 0), ("v", 1, 1)], 5: [("v", 1, 2), ("v", 1, 3)],
    8: [("out", 0)], 9: [("mean", 0)], 10: [("var", 0)], 11: [("gate", 0), ("fv", 0)],
    13: [("out", 1)], 14: [("mean", 1)], 15: [("var", 1)], 16: [("gate", 1), ("fv", 1), ("out2", 0)],
    17: [("mean2", 0)], 18: [("var2", 0)], 20: [("out2", 1)], 21: [("mean2", 1)], 22: [("var2", 1)],
}
ITERATIONS = 23
SEQ = {}
for _i, _e in enumerate(LINE):
    if _e is not None:
        SEQ[_i] = len(SEQ)
ENTRY_OF = {LINE[_i]: _s for _i, _s in SEQ.items()}
entries = [LINE[_i] for _i in SEQ]


def vit_tower(nc, x_t, tok_w, w_qk, w_v, w_out, f_qk, f_v, f_g1, f_g2, f_p01, f_p2, pos_bias,
              biases, consts, bf_consts, out_t):
    with ExitStack() as ctx:
        def sb(name, shape, dt=F32):
            return ctx.enter_context(nc.sbuf_tensor(name, shape, dt))

        def sem(name):
            return ctx.enter_context(nc.semaphore(name))

        x_f = sb("x_f", [128, PK, IMAGES * TOK])
        x_hi = sb("x_hi", [128, PK, IMAGES * TOK], F32R)
        x_lo = sb("x_lo", [128, PK, IMAGES * TOK], F32R)
        tw_f = sb("tw_f", [128, PK, DIM])
        tw_hi = sb("tw_hi", [128, PK, DIM], F32R)
        tw_lo = sb("tw_lo", [128, PK, DIM], F32R)
        wqk_f = sb("wqk_f", [128, PAIRS, NCH, 256])
        wqk_hi = sb("wqk_hi", [CH, PAIRS, NCH, 256], F32R)
        wqk_lo = sb("wqk_lo", [CH, PAIRS, NCH, 256], F32R)
        wv_f = sb("wv_f", [128, NCH, PATCH])
        wv_hi = sb("wv_hi", [CH, NCH, PATCH], F32R)
        wv_lo = sb("wv_lo", [CH, NCH, PATCH], F32R)
        wo_f = sb("wo_f", [128, PAIRS, DIM])
        wo_hi = sb("wo_hi", [128, PAIRS, DIM], F32R)
        wo_lo = sb("wo_lo", [128, PAIRS, DIM], F32R)
        fqk_w = sb("fqk_w", [CH, NCH, 512])
        fv_w = sb("fv_w", [CH + 1, NCH, DIM])
        fg1_w = sb("fg1_w", [CH, NCH, 32])
        fg2_w = sb("fg2_w", [33, 3])
        fp01_w = sb("fp01_w", [128, DIM])
        fp2_w = sb("fp2_w", [HD, DIM])
        bias = sb("bias", [128, B_END])
        const = sb("const", [128, C_END])
        bfc = sb("bfc", [128, 128 + 2 * TOK], BF16)
        posb = sb("posb", [128, TOK])
        posmask = sb("posmask", [128, TOK])
        ident = const[:, C_IDENT:C_IDENT + 128]
        outside = const[:, C_OUTSIDE:C_OUTSIDE + 1]
        eps = const[0:CH, C_EPS:C_EPS + 1]
        mean_w = const[0:CH, C_MEAN:C_MEAN + CH]
        ident_bf = bfc[:, 0:128]
        band_bf = bfc[:, 128:128 + TOK]
        causal_bf = bfc[:, 128 + TOK:128 + 2 * TOK]

        h_f = sb("h_f", [CH, NCH, IMAGES, TOK])
        h_hi = sb("h_hi", [CH, NCH, IMAGES, SLOT], F32R)
        h_lo = sb("h_lo", [CH, NCH, IMAGES, SLOT], F32R)
        n_seq = len(SEQ)
        q_t = sb("q_t", [128, QK_RING, GT])
        k_t = sb("k_t", [128, QK_RING, GT])
        qc_t = sb("qc_t", [HD, GROUPS, 2, GT])
        v_t = [sb("v_t", [128, TILES, PATCH])[:],
               x_f[:].rearrange("p k t -> p (k t)")[:, 0:TILES * PATCH].rearrange("p (j d) -> p j d", d=PATCH)]
        fv_t = wv_f[:].rearrange("p c (j d) -> p (c j) d", d=DIM)
        d_t = sb("d_t", [128, 2, GI, TOK])
        e_t = sb("e_t", [128, 2, GI, TOK])
        p_t = sb("p_t", [128, 2, GI, SLOT])
        pt_t = sb("pt_t", [128, 2, TILES, 2, TOK])
        mx_t = sb("mx_t", [128, n_seq, 2, GI])
        z_t = sb("z_t", [128, n_seq, GI])
        sm_t = sb("sm_t", [128, n_seq, 3, GI])
        o_hi = x_hi[:].rearrange("p k (g t) -> p g k t", g=GROUPS)
        o_lo = x_lo[:].rearrange("p k (g t) -> p g k t", g=GROUPS)
        r_t = sb("r_t", [CH, NCH, GT])
        c_t = sb("c_t", [CH, NCH, GT])
        sq_t = sb("sq_t", [CH, NCH, GT])
        ln_t = sb("ln_t", [CH, 2, GT])
        freed_qk = wqk_f[:].rearrange("p a c d -> p (a c d)")
        n_h1 = GROUPS * NCH * GI * SLOT
        h1 = freed_qk[0:CH + 1, 0:n_h1].rearrange("p (g c i s) -> p g c i s", g=GROUPS, c=NCH, s=SLOT)
        g1_t = freed_qk[0:33, n_h1:n_h1 + GI * 2 * SLOT].rearrange("p (i d s) -> p i d s", d=2, s=SLOT)
        gm = sb("gm", [128, GROUPS, 10, GI, 3])
        gs = sb("gs", [128, GROUPS, 8, GI])
        wgt = sb("wgt", [128, GROUPS, 2, GI])
        y01 = sb("y01", [128, GROUPS, GT])
        y2 = sb("y2", [HD, GROUPS, GT])
        out_s = tw_f[0:CH].rearrange("p k d -> p (k d)").rearrange("p (g c t) -> p g c t", g=GROUPS, c=NCH)

        proj = [ctx.enter_context(nc.psum_tensor(f"proj{i}", [128, 512], F32)) for i in range(3)]
        score = [ctx.enter_context(nc.psum_tensor(f"score{i}", [128, 512], F32)) for i in range(2)]
        trans = ctx.enter_context(nc.psum_tensor("trans", [128, TILES, 2, SLOT], F32))
        outp = ctx.enter_context(nc.psum_tensor("outp", [128, 2, 512], F32))
        embed_bank = [[proj[0], proj[1]], [score[0], score[1]]]

        ld_const, ld_tok, ld_wv, ld_wo, ld_ffn = (sem(s) for s in ("ld_const", "ld_tok", "ld_wv", "ld_wo", "ld_ffn"))
        ld_x = [sem(f"ld_x{k}") for k in range(PK)]
        ld_qk = [sem(f"ld_qk{p}") for p in range(PAIRS)]
        ld_bias = sem("ld_bias")
        st_out = sem("st_out")
        zeroed2 = sem("zeroed2")
        zeroed = sem("zeroed")
        tok_hi, tok_lo, x_hi_s, x_lo_s = (sem(s) for s in ("tok_hi", "tok_lo", "x_hi_s", "x_lo_s"))
        qk_hi, qk_lo, wv_hi_s, wv_lo_s, wo_hi_s, wo_lo_s = (
            sem(s) for s in ("qk_hi", "qk_lo", "wv_hi_s", "wv_lo_s", "wo_hi_s", "wo_lo_s"))
        posmask_s = sem("posmask_s")
        embedded = sem("embedded")
        h_hi_s, h_f_s, h_lo_s = (sem(s) for s in ("h_hi_s", "h_f_s", "h_lo_s"))
        projected = sem("projected")
        scored = sem("scored")
        transposed = sem("transposed")
        attended = sem("attended")
        q_s, k_s = sem("q_s"), sem("k_s")
        v_act, v_dve = sem("v_act"), sem("v_dve")
        shifted, exped, zeroed_key, normed, pt_s = (
            sem(s) for s in ("shifted", "exped", "outside_exped", "normed", "pt_s"))
        o_hi_s, o_lo_s = sem("o_hi_s"), sem("o_lo_s")
        res_s, cen_s, sq_s, rstd_s, h1_s = (sem(s) for s in ("res_s", "cen_s", "sq_s", "rstd_s", "h1_s"))
        g1_s, gate_exp, gate_exp2, gated, conv_s, fv_s = (
            sem(s) for s in ("g1_s", "gate_exp", "gate_exp2", "gated", "conv_s", "fv_s"))
        gate_d, gate_g, logit_s = sem("gate_d"), sem("gate_g"), sem("logit_s")
        outs_half, outs = sem("outs_half"), sem("outs")
        dve_chain, act_chain = sem("dve_chain"), sem("act_chain")

        uses, freed_by = {}, []

        def plan(kind, key, freed):
            uses[(kind, key)] = len(freed_by)
            freed_by.append(freed)

        n_res = n_stat = n_v = 0
        for i in range(ITERATIONS):
            if i in SEQ:
                plan("q", SEQ[i], (q_s, SEQ[i] + 1))
                plan("k", SEQ[i], (k_s, SEQ[i] + 1))
            for step in STEPS.get(i, ()):
                kind, g = step[0], step[1]
                if kind == "v":
                    n_v += 1
                    plan("v", (g, step[2], 0), (v_act, n_v))
                    plan("v", (g, step[2], 1), (v_dve, n_v))
                elif kind in ("out", "out2"):
                    for m in range(NCH):
                        n_res += 1
                        plan(kind, (g, m), (res_s, n_res))
                elif kind in ("mean", "mean2"):
                    plan(kind, g, (cen_s, len([u for u in uses if u[0] in ("mean", "mean2")]) + 1))
                elif kind in ("var", "var2"):
                    n_stat += 1
                    plan(kind, g, (act_chain, None))
                elif kind == "gate":
                    plan("g1", g, (g1_s, g + 1))
                elif kind == "fv":
                    plan("fv", (g, 0), (fv_s, 2 * g + 1))
                    plan("fv", (g, 1), (fv_s, 2 * g + 2))
                    plan("lg", g, (logit_s, g + 1))
        ln_order = [(s[0], s[1]) for i in range(ITERATIONS) for s in STEPS.get(i, ()) if s[0] in ("var", "var2")]
        ln_index = {s: n for n, s in enumerate(ln_order)}
        for (kind, key), n in list(uses.items()):
            if kind in ("var", "var2"):
                freed_by[n] = (rstd_s, ln_index[(kind, key)] + 1)
        norm_of = {("out", 0): ("var", 0), ("out", 1): ("var", 1), ("out2", 0): ("var2", 0), ("out2", 1): ("var2", 1)}

        def bank(kind, key):
            return proj[uses[(kind, key)] % 3]

        def hcols(t, g, c):
            return t[:, c, GI * g:GI * g + GI, 0:TOK]

        def by_image(ap):
            return ap.rearrange("p (i t) -> p i t", t=TOK)

        ZEROED, ZEROED2 = 4, 4
        block = ctx.enter_context(nc.Block())

        @block.sync
        def _(sp):
            sp.dma_start(tw_f[:], tok_w).then_inc(ld_tok, 16)
            for k in range(PK):
                sp.dma_start(x_f[:, k, :], x_t[:, k, :]).then_inc(ld_x[k], 16)
            for p in range(PAIRS):
                sp.dma_start(wqk_f[0:CH, p], w_qk[:, p]).then_inc(ld_qk[p], 16)
            sp.dma_start(wo_f[:], w_out).then_inc(ld_wo, 16)
            for n, g in enumerate((0, 1)):
                sp.wait_ge(outs, n + 1)
                sp.dma_start(out_t[:, :, g * GT:(g + 1) * GT], out_s[:, g]).then_inc(st_out, 16)
            sp.wait_ge(st_out, 16 * GROUPS)

        @block.gpsimd
        def _(pool):
            for t in (h_hi, h_lo, p_t, posb):
                pool.memset(t[:].bitcast(F32), 0.0).then_inc(zeroed, 1)
            for p in range(PAIRS):
                pool.wait_ge(qk_hi, p + 1)
                nc.gpsimd.tensor_tensor(wqk_lo[:, p], wqk_f[0:CH, p], wqk_hi[:, p].bitcast(F32),
                                        ALU.subtract).then_inc(qk_lo, 1)
            pool.wait_ge(qk_lo, PAIRS)
            pool.memset(h1, 0.0).then_inc(zeroed2, 1)
            pool.memset(g1_t, 0.0).then_inc(zeroed2, 1)
            pool.wait_ge(zeroed2, 2)
            pool.memset(h1[CH:CH + 1], 1.0).then_inc(zeroed2, 1)
            pool.memset(g1_t[32:33], 1.0).then_inc(zeroed2, 1)
            pool.wait_ge(zeroed2, ZEROED2)
            pool.wait_ge(wo_hi_s, 1)
            nc.gpsimd.tensor_tensor(wo_lo[:], wo_f[:], wo_hi[:].bitcast(F32), ALU.subtract).then_inc(wo_lo_s, 1)


        @block.scalar
        def _(act):
            act.dma_start(bias[:], biases).then_inc(ld_bias, 16)
            act.dma_start(const[:], consts).then_inc(ld_const, 16)
            act.dma_start(bfc[:], bf_consts).then_inc(ld_const, 16)
            act.dma_start(wv_f[0:CH], w_v).then_inc(ld_wv, 16)
            act.dma_start(fqk_w[:], f_qk).then_inc(ld_ffn, 16)
            act.dma_start(fv_w[:], f_v).then_inc(ld_ffn, 16)
            act.dma_start(fg1_w[:], f_g1).then_inc(ld_ffn, 16)
            act.dma_start(fg2_w[:], f_g2).then_inc(ld_ffn, 16)
            act.dma_start(fp01_w[:], f_p01).then_inc(ld_ffn, 16)
            act.dma_start(fp2_w[:], f_p2).then_inc(ld_ffn, 16)
            act.wait_ge(zeroed, ZEROED)
            for half in range(2):
                act.dma_start(posb[64 * half:64 * half + TOK, :], pos_bias).then_inc(ld_ffn, 16)
            act.preload_act_table_set("natural_log_exp_and_others")

            act.wait_ge(ld_tok, 16)
            nc.scalar.activation(tw_hi[:], tw_f[:], ACT.Copy).then_inc(tok_hi, 1)
            for k in range(PK):
                act.wait_ge(ld_x[k], 16)
                nc.scalar.activation(x_hi[:, k], x_f[:, k], ACT.Copy).then_inc(x_hi_s, 1)
            for p in range(PAIRS):
                act.wait_ge(ld_qk[p], 16)
                nc.scalar.activation(wqk_hi[:, p], wqk_f[0:CH, p], ACT.Copy).then_inc(qk_hi, 1)
                if p == 1:
                    act.wait_ge(ld_wv, 16)
                    nc.scalar.activation(wv_hi[:], wv_f[0:CH], ACT.Copy).then_inc(wv_hi_s, 1)
            act.wait_ge(ld_bias, 16)
            for n, (g, m) in enumerate((g, m) for g in range(GROUPS) for m in range(NCH)):
                act.wait_ge(embedded, n + 1)
                nc.scalar.activation(hcols(h_hi, g, m), by_image(embed_bank[g][m][0:CH, 0:GT]), ACT.Identity,
                                     bias=bias[0:CH, B_TOK + m:B_TOK + m + 1]).then_inc(h_hi_s, 1)

            def copy_q_k(n):
                kind, g, p = entries[n]
                if n >= QK_RING:
                    act.wait_ge(scored, n - QK_RING + 1)
                for which, (dst, name, done) in enumerate(((q_t, "q", q_s), (k_t, "k", k_s))):
                    act.wait_ge(projected, uses[(name, n)] + 1)
                    b = bank(name, n)[:, 0:GT]
                    if kind == "attn":
                        nc.scalar.activation(dst[:, n % QK_RING], b, ACT.Copy).then_inc(done, 1)
                    else:
                        col = B_QK + 2 * p + which
                        nc.scalar.activation(dst[:, n % QK_RING], b, ACT.Identity, bias=bias[:, col:col + 1]).then_inc(done, 1)

            def exp_scores(n):
                if n >= 2:
                    act.wait_ge(normed, n - 1)
                act.wait_ge(shifted, n + 1)
                nc.scalar.activation(e_t[:, n % 2], d_t[:, n % 2], ACT.Exp, scale=SCALE).then_inc(exped, 1)
                if entries[n][0] == "attn":
                    nc.scalar.activation(z_t[:, n], mx_t[:, n, 1], ACT.Exp, scale=-SCALE).then_inc(zeroed_key, 1)

            def copy_transposed(n):
                act.wait_ge(transposed, n + 1)
                if n >= 2:
                    act.wait_ge(attended, n - 1)
                nc.scalar.activation(pt_t[:, n % 2], trans[:, :, :, 0:TOK], ACT.Copy).then_inc(pt_s, 1)

            def copy_outputs(n):
                kind, g, p = entries[n]
                act.wait_ge(attended, n + 1)
                rows = 128 if (kind, p) != ("ffn", 1) else HD
                src = outp[0:rows, :, 0:GT // 2].rearrange("p h (j t) -> p h j t", t=TOK)
                dst = o_hi[:, g, p] if kind == "attn" else y01[:, g] if p == 0 else y2[:, g]
                dst = dst.rearrange("p (j h t) -> p h j t", h=2, t=TOK)
                nc.scalar.activation(dst, src, ACT.Copy).then_inc(o_hi_s, 1)

            def step(s):
                kind, g = s[0], s[1]
                if kind == "v":
                    u = (g, s[2], 0)
                    act.wait_ge(projected, uses[("v", u)] + 1)
                    nc.scalar.activation(v_t[g][:, s[2], 0:384], bank("v", u)[:, 0:384],
                                         ACT.Copy).then_inc(v_act, 1)
                elif kind in ("mean", "mean2"):
                    n = ln_index[(kind.replace("mean", "var"), g)]
                    act.wait_ge(cen_s, n + 1)
                    nc.scalar.activation(sq_t[:], c_t[:], ACT.Square).then_inc(sq_s, 1)
                elif kind in ("var", "var2"):
                    n = ln_index[(kind, g)]
                    act.wait_ge(projected, uses[(kind, g)] + 1)
                    nc.scalar.activation(ln_t[:, 0], bank(kind, g)[0:CH, 0:GT], ACT.Ln, bias=eps).then_inc(act_chain, 1)
                    act.wait_ge(act_chain, n + 1)
                    nc.scalar.activation(ln_t[:, 1], ln_t[:, 0], ACT.Exp, scale=-0.5).then_inc(rstd_s, 1)
                elif kind == "gate":
                    act.wait_ge(projected, uses[("g1", g)] + 1)
                    src = by_image(bank("g1", g)[0:32, 0:GT])
                    act.wait_ge(zeroed2, ZEROED2)
                    if g:
                        act.wait_ge(logit_s, g)
                    for dup in range(2):
                        nc.scalar.activation(g1_t[0:32, :, dup, 0:TOK], src, ACT.Relu,
                                             bias=bias[0:32, B_G1:B_G1 + 1]).then_inc(g1_s, 1)
                elif kind == "fv":
                    act.wait_ge(gate_d, g + 1)
                    nc.scalar.activation(gm[:, g, 1], gm[:, g, 0], ACT.Exp).then_inc(gate_exp, 1)
                    act.wait_ge(gate_g, g + 1)
                    nc.scalar.activation(gm[:, g, 4], gm[:, g, 3], ACT.Exp).then_inc(gate_exp2, 1)

            for i in range(ITERATIONS):
                if i - 2 in SEQ:
                    copy_transposed(SEQ[i - 2])
                if i - 1 in SEQ:
                    exp_scores(SEQ[i - 1])
                if i in SEQ:
                    copy_q_k(SEQ[i])
                if i - 2 in SEQ:
                    copy_outputs(SEQ[i - 2])
                if i == 1:
                    act.wait_ge(ld_wo, 16)
                    nc.scalar.activation(wo_hi[:], wo_f[:], ACT.Copy).then_inc(wo_hi_s, 1)
                for s in STEPS.get(i, ()):
                    step(s)

        @block.vector
        def _(dve):
            chain = [0]

            def link(ins):
                chain[0] += 1
                ins.then_inc(dve_chain, 1)
                dve.wait_ge(dve_chain, chain[0])

            dve.wait_ge(tok_hi, 1)
            nc.vector.tensor_tensor(tw_lo[:], tw_f[:], tw_hi[:].bitcast(F32), ALU.subtract).then_inc(tok_lo, 1)
            for k in range(PK):
                dve.wait_ge(x_hi_s, k + 1)
                nc.vector.tensor_tensor(x_lo[:, k], x_f[:, k], x_hi[:, k].bitcast(F32),
                                        ALU.subtract).then_inc(x_lo_s, 1)
            dve.wait_ge(wv_hi_s, 1)
            nc.vector.tensor_tensor(wv_lo[:], wv_f[0:CH], wv_hi[:].bitcast(F32), ALU.subtract).then_inc(wv_lo_s, 1)
            dve.wait_ge(ld_ffn, 16 * 8)
            dve.wait_ge(ld_const, 32)
            nc.vector.scalar_tensor_tensor(out=posmask[:], in0=posb[:], scalar=1.0 / SCALE,
                                           in1=const[:, C_CAUSAL:C_CAUSAL + TOK], op0=ALU.mult,
                                           op1=ALU.add).then_inc(posmask_s, 1)
            dve.wait_ge(ld_bias, 16)
            for n, (g, m) in enumerate((g, m) for g in range(GROUPS) for m in range(NCH)):
                dve.wait_ge(h_hi_s, n + 1)
                nc.vector.tensor_scalar(hcols(h_f, g, m), by_image(embed_bank[g][m][0:CH, 0:GT]),
                                        bias[0:CH, B_TOK + m:B_TOK + m + 1], None, ALU.add).then_inc(h_f_s, 1)
                dve.wait_ge(h_f_s, n + 1)
                nc.vector.tensor_tensor(hcols(h_lo, g, m), hcols(h_f, g, m), hcols(h_hi, g, m).bitcast(F32),
                                        ALU.subtract).then_inc(h_lo_s, 1)

            def softmax(n):
                kind, g, p = entries[n]
                s = by_image(score[n % 2][:, 0:GT])
                dve.wait_ge(scored, n + 1)
                if kind == "attn":
                    link(nc.vector.tensor_reduce(mx_t[:, n, 0], s, AX.X, ALU.max))
                    link(nc.vector.tensor_scalar(mx_t[:, n, 1], mx_t[:, n, 0], 0.0, None, ALU.max))
                else:
                    link(nc.vector.tensor_reduce(mx_t[:, n, 1], s, AX.X, ALU.max))
                if n >= 2:
                    dve.wait_ge(exped, n - 1)
                nc.vector.tensor_tensor(d_t[:, n % 2], s, mx_t[:, n, 1].unsqueeze(2).broadcast_to([128, GI, TOK]),
                                        ALU.subtract).then_inc(shifted, 1)
                dve.wait_ge(exped, n + 1)
                link(nc.vector.tensor_reduce(sm_t[:, n, 0], e_t[:, n % 2], AX.X, ALU.add))
                if kind == "attn":
                    dve.wait_ge(zeroed_key, n + 1 if n < 12 else 12)
                    link(nc.vector.scalar_tensor_tensor(out=sm_t[:, n, 1], in0=z_t[:, n], scalar=outside,
                                                        in1=sm_t[:, n, 0], op0=ALU.mult, op1=ALU.add))
                    link(nc.vector.reciprocal(sm_t[:, n, 2], sm_t[:, n, 1]))
                else:
                    link(nc.vector.reciprocal(sm_t[:, n, 1], sm_t[:, n, 0]))
                    dve.wait_ge(gated, 3 * g + 3)
                    link(nc.vector.tensor_tensor(sm_t[:, n, 2], sm_t[:, n, 1], wgt[:, g, p], ALU.mult))
                if n >= 2:
                    dve.wait_ge(transposed, n - 1)
                nc.vector.tensor_tensor(p_t[:, n % 2, :, 0:TOK], e_t[:, n % 2],
                                        sm_t[:, n, 2].unsqueeze(2).broadcast_to([128, GI, TOK]),
                                        ALU.mult).then_inc(normed, 1)

            def outputs_lo(n):
                kind, g, p = entries[n]
                if kind != "attn":
                    return
                dve.wait_ge(o_hi_s, n + 1)
                src = outp[:, :, 0:GT // 2].rearrange("p h (j t) -> p h j t", t=TOK)
                hi = o_hi[:, g, p].rearrange("p (j h t) -> p h j t", h=2, t=TOK)
                lo = o_lo[:, g, p].rearrange("p (j h t) -> p h j t", h=2, t=TOK)
                nc.vector.tensor_tensor(lo, src, hi.bitcast(F32), ALU.subtract).then_inc(o_lo_s, 1)

            def convolve(n):
                g = entries[n][1]
                dve.wait_ge(q_s, n + 1)
                q = by_image(q_t[0:HD, n % QK_RING])
                a, b = (by_image(qc_t[:, g, z]) for z in range(2))
                w = [bias[0:HD, B_CONVW + j:B_CONVW + j + 1] for j in range(3)]
                link(nc.vector.tensor_scalar(a, q, w[1], bias[0:HD, B_CONVB:B_CONVB + 1], ALU.mult, ALU.add))
                nc.vector.tensor_copy(b[:, :, 0:1], a[:, :, 0:1])
                link(nc.vector.scalar_tensor_tensor(out=b[:, :, 1:TOK], in0=q[:, :, 0:TOK - 1], scalar=w[0],
                                                    in1=a[:, :, 1:TOK], op0=ALU.mult, op1=ALU.add))
                link(nc.vector.tensor_copy(a[:, :, TOK - 1:TOK], b[:, :, TOK - 1:TOK]))
                nc.vector.scalar_tensor_tensor(out=a[:, :, 0:TOK - 1], in0=q[:, :, 1:TOK], scalar=w[2],
                                               in1=b[:, :, 0:TOK - 1], op0=ALU.mult, op1=ALU.add).then_inc(conv_s, 1)

            def gate(g):
                t = [gm[:, g, z] for z in range(10)]
                s = [gs[:, g, z] for z in range(8)]
                wide = lambda z: z.unsqueeze(2).broadcast_to([128, GI, 3])
                dve.wait_ge(projected, uses[("lg", g)] + 1)
                lg = bank("lg", g)[:, 0:3 * GI].rearrange("p (i e) -> p i e", e=3)
                link(nc.vector.tensor_reduce(s[0], lg, AX.X, ALU.max))
                link(nc.vector.tensor_tensor(t[0], lg, wide(s[0]), ALU.subtract))
                dve.sem_inc(gate_d, 1)
                dve.sem_inc(logit_s, 1)
                dve.wait_ge(gate_exp, g + 1)
                link(nc.vector.tensor_reduce(s[1], t[1], AX.X, ALU.add))
                link(nc.vector.reciprocal(s[2], s[1]))
                link(nc.vector.tensor_tensor(t[2], t[1], wide(s[2]), ALU.mult))
                link(nc.vector.tensor_reduce(s[3], t[2], AX.X, ALU.max))
                nc.vector.tensor_tensor(t[3], t[2], wide(s[3]), ALU.subtract).then_inc(gate_g, 1)
                g0, g1, g2 = (t[2][:, :, z] for z in range(3))
                nc.vector.tensor_tensor(s[4], g0, g1, ALU.min)
                link(nc.vector.tensor_tensor(s[5], g1, g2, ALU.min))
                keep = t[5]
                nc.vector.tensor_tensor(keep[:, :, 2], g2, s[4], ALU.is_gt)
                link(nc.vector.tensor_tensor(keep[:, :, 0], g0, s[5], ALU.is_ge))
                link(nc.vector.tensor_tensor(s[6], keep[:, :, 0], keep[:, :, 2], ALU.add))
                link(nc.vector.tensor_scalar(keep[:, :, 1], s[6], -1.0, 2.0, ALU.mult, ALU.add))
                dve.wait_ge(gate_exp2, g + 1)
                link(nc.vector.tensor_tensor(t[6], t[4], keep, ALU.mult))
                link(nc.vector.tensor_reduce(s[7], t[6], AX.X, ALU.add))
                link(nc.vector.reciprocal(s[0], s[7]))
                link(nc.vector.tensor_tensor(t[7], t[6], wide(s[0]), ALU.mult))
                nc.vector.tensor_copy(wgt[0:64, g, 0], t[7][0:64, :, 0]).then_inc(gated, 1)
                nc.vector.tensor_copy(wgt[64:128, g, 0], t[7][64:128, :, 1]).then_inc(gated, 1)
                nc.vector.tensor_copy(wgt[:, g, 1], t[7][:, :, 2]).then_inc(gated, 1)

            def step(s):
                kind, g = s[0], s[1]
                if kind == "v":
                    u = (g, s[2], 1)
                    dve.wait_ge(projected, uses[("v", u)] + 1)
                    nc.vector.tensor_copy(v_t[g][:, s[2], 384:768],
                                          bank("v", u)[:, 0:384]).then_inc(v_dve, 1)
                elif kind in ("out", "out2"):
                    n = ln_index[norm_of[(kind, g)]]
                    if n:
                        dve.wait_ge(cen_s, n)
                    for m in range(NCH):
                        dve.wait_ge(projected, uses[(kind, (g, m))] + 1)
                        if kind == "out":
                            b, res = bias[0:CH, B_OUT + m:B_OUT + m + 1], hcols(h_f, g, m)
                        else:
                            b, res = bias[0:CH, B_FFN + m:B_FFN + m + 1], h1[0:CH, g, m, :, 0:TOK]
                        nc.vector.scalar_tensor_tensor(out=by_image(r_t[:, m]),
                                                       in0=by_image(bank(kind, (g, m))[0:CH, 0:GT]), scalar=b,
                                                       in1=res, op0=ALU.add, op1=ALU.add).then_inc(res_s, 1)
                elif kind in ("mean", "mean2"):
                    n = ln_index[(kind.replace("mean", "var"), g)]
                    dve.wait_ge(projected, uses[(kind, g)] + 1)
                    if n:
                        dve.wait_ge(sq_s, n)
                    nc.vector.tensor_tensor(c_t[:], r_t[:], bank(kind, g)[0:CH, 0:GT].unsqueeze(1)
                                            .broadcast_to([CH, NCH, GT]), ALU.subtract).then_inc(cen_s, 1)
                elif kind in ("var", "var2"):
                    n = ln_index[(kind, g)]
                    dve.wait_ge(rstd_s, n + 1)
                    dve.wait_ge(zeroed2, ZEROED2)
                    for m in range(NCH):
                        dst = h1[0:CH, g, m, :, 0:TOK] if kind == "var" else by_image(out_s[:, g, m])
                        ins = nc.vector.tensor_tensor(dst, by_image(c_t[:, m]), by_image(ln_t[:, 1]), ALU.mult)
                        ins.then_inc(h1_s if kind == "var" else outs_half, 1)
                    if kind == "var2":
                        dve.wait_ge(outs_half, 2 * g + 2)
                        dve.sem_inc(outs, 1)
                elif kind == "fv":
                    for z in range(2):
                        dve.wait_ge(projected, uses[("fv", (g, z))] + 1)
                        src = bank("fv", (g, z))[:, 0:2 * DIM].rearrange("p (j d) -> p j d", d=DIM)
                        nc.vector.tensor_copy(fv_t[:, TILES * g + 2 * z:TILES * g + 2 * z + 2], src).then_inc(fv_s, 1)
                    gate(g)

            for i in range(ITERATIONS):
                if i - 1 in SEQ:
                    softmax(SEQ[i - 1])
                if i in SEQ and LINE[i][0] == "ffn" and LINE[i][2] == 0:
                    convolve(SEQ[i])
                if i - 2 in SEQ:
                    outputs_lo(SEQ[i - 2])
                for s in STEPS.get(i, ()):
                    step(s)

        @block.tensor
        def _(pe):
            def split_matmul(out, pairs, last=True):
                ops = [(a, b) for (ah, al), (bh, bl) in pairs for a, b in ((ah, bh), (ah, bl), (al, bh))]
                for n, (a, b) in enumerate(ops):
                    ins = nc.tensor.matmul(out, a, b, start=(n == 0), stop=(n == len(ops) - 1))
                return ins

            def take(kind, key):
                n = uses[(kind, key)]
                if n >= 3:
                    pe.wait_ge(*freed_by[n - 3])
                return proj[n % 3]

            pe.wait_ge(tok_lo, 1)
            for k in range(PK):
                pe.wait_ge(x_lo_s, k + 1)
                for g in range(GROUPS):
                    cols = slice(g * GT, (g + 1) * GT)
                    for m in range(NCH):
                        rows = slice(CH * m, CH * m + CH)
                        for n, (a, b) in enumerate(((tw_hi, x_hi), (tw_hi, x_lo), (tw_lo, x_hi))):
                            ins = nc.tensor.matmul(embed_bank[g][m][0:CH, 0:GT], a[:, k, rows], b[:, k, cols],
                                                   start=(k == 0 and n == 0), stop=(k == PK - 1 and n == 2))
                        if k == PK - 1:
                            ins.then_inc(embedded, 1)
            pe.wait_ge(zeroed, ZEROED)
            pe.wait_ge(ld_const, 32)

            def project_qk(n):
                kind, g, p = entries[n]
                if kind == "attn":
                    pe.wait_ge(qk_lo, p + 1)
                    pe.wait_ge(h_lo_s, 2 * GROUPS)
                    pe.wait_ge(h_hi_s, 2 * GROUPS)
                    for which, name in enumerate("qk"):
                        b = take(name, n)
                        cols = slice(128 * which, 128 * which + 128)
                        split_matmul(by_image(b[:, 0:GT]),
                                     [((wqk_hi[:, p, c, cols], wqk_lo[:, p, c, cols]),
                                       (hcols(h_hi, g, c), hcols(h_lo, g, c))) for c in range(NCH)]
                                     ).then_inc(projected, 1)
                else:
                    pe.wait_ge(h1_s, 2 * g + 2)
                    pe.wait_ge(ld_ffn, 16 * 8)
                    for which, name in enumerate("qk"):
                        b = take(name, n)
                        col = 128 * (2 * p + which)
                        for c in range(NCH):
                            ins = nc.tensor.matmul(by_image(b[:, 0:GT]), fqk_w[:, c, col:col + 128],
                                                   h1[0:CH, g, c, :, 0:TOK], start=(c == 0), stop=(c == NCH - 1))
                        ins.then_inc(projected, 1)

            def scores(n):
                kind, g, p = entries[n]
                out = by_image(score[n % 2][:, 0:GT])
                pe.wait_ge(k_s, n + 1)
                pe.wait_ge(q_s, n + 1)
                if n >= 2:
                    pe.wait_ge(shifted, n - 1)
                if (kind, p) == ("ffn", 0):
                    pe.wait_ge(conv_s, g + 1)
                if (kind, p) == ("ffn", 1):
                    pe.wait_ge(posmask_s, 1)
                    idn, mask = ident, posmask[:]
                else:
                    idn, mask = ident_bf, band_bf if kind == "attn" else causal_bf
                nc.tensor.matmul(out, idn, mask.unsqueeze(1).broadcast_to([128, GI, TOK]), start=True, stop=False,
                                 skip_group_check=True)
                for im in range(GI):
                    cols = slice(TOK * im, TOK * im + TOK)
                    for h in range(2):
                        rows = slice(HD * h, HD * h + HD)
                        q = qc_t[:, g, 0, cols] if (kind, p, h) == ("ffn", 0, 0) else q_t[rows, n % QK_RING, cols]
                        ins = nc.tensor.matmul(score[n % 2][64 * h:64 * h + TOK, cols], q, k_t[rows, n % QK_RING, cols],
                                               start=False, stop=True, skip_group_check=True)
                ins.then_inc(scored, 1)

            def transposes(n):
                pe.wait_ge(normed, n + 1)
                if n >= 1:
                    pe.wait_ge(pt_s, n)
                for j in range(TILES):
                    src = p_t[:, n % 2, 2 * j:2 * j + 2, :].rearrange("p i s -> p (i s)")
                    ins = nc.tensor.transpose(trans[:, j].rearrange("p h s -> p (h s)"), src, ident)
                ins.then_inc(transposed, 1)

            def outputs(n):
                kind, g, p = entries[n]
                pe.wait_ge(pt_s, n + 1)
                if n >= 1:
                    pe.wait_ge(o_hi_s, n)
                    pe.wait_ge(o_lo_s, min(n, 12))
                if kind == "attn":
                    pe.wait_ge(v_act, TILES * g + TILES)
                    pe.wait_ge(v_dve, TILES * g + TILES)
                else:
                    pe.wait_ge(fv_s, 2 * g + 2)
                heads = 1 if (kind, p) == ("ffn", 1) else 2
                val = v_t[g] if kind == "attn" else fv_t[:, TILES * g:TILES * g + TILES]
                for j in range(TILES):
                    for half in range(2):
                        keys = slice(64 * half, 64 * half + TOK)
                        for h in range(heads):
                            d = HD * (2 * p + h)
                            ins = nc.tensor.matmul(outp[HD * h:HD * h + HD, half, TOK * j:TOK * j + TOK],
                                                   val[keys, j, d:d + HD], pt_t[keys, n % 2, j, h, :],
                                                   start=True, stop=True)
                ins.then_inc(attended, 1)

            def step(s):
                kind, g = s[0], s[1]
                if kind == "v":
                    pe.wait_ge(wv_lo_s, 1)
                    for half in range(2):
                        b = take("v", (g, s[2], half))
                        im, cols = GI * g + 2 * s[2], slice(384 * half, 384 * half + 384)
                        tile = lambda t, c: t[:, c, im:im + 2, :].rearrange("p i s -> p (i s)")
                        split_matmul(b[:, 0:384], [((tile(h_hi, c), tile(h_lo, c)),
                                                    (wv_hi[:, c, cols], wv_lo[:, c, cols])) for c in range(NCH)]
                                     ).then_inc(projected, 1)
                elif kind == "out":
                    pe.wait_ge(wo_lo_s, 1)
                    pe.wait_ge(o_lo_s, PAIRS * g + PAIRS)
                    for m in range(NCH):
                        b = take("out", (g, m))
                        rows = slice(CH * m, CH * m + CH)
                        split_matmul(b[0:CH, 0:GT], [((wo_hi[:, p, rows], wo_lo[:, p, rows]),
                                                      (o_hi[:, g, p], o_lo[:, g, p])) for p in range(PAIRS)]
                                     ).then_inc(projected, 1)
                elif kind == "out2":
                    pe.wait_ge(o_hi_s, ENTRY_OF[("ffn", g, 1)] + 1)
                    for m in range(NCH):
                        b = take("out2", (g, m))
                        rows = slice(CH * m, CH * m + CH)
                        nc.tensor.matmul(b[0:CH, 0:GT], fp01_w[:, rows], y01[:, g], start=True, stop=False)
                        nc.tensor.matmul(b[0:CH, 0:GT], fp2_w[:, rows], y2[:, g], start=False,
                                         stop=True).then_inc(projected, 1)
                elif kind in ("mean", "mean2", "var", "var2"):
                    n = ln_index[(kind.replace("mean", "var"), g)]
                    if kind.startswith("mean"):
                        pe.wait_ge(res_s, 2 * n + 2)
                        src = r_t
                    else:
                        pe.wait_ge(sq_s, n + 1)
                        src = sq_t
                    b = take(kind, g)
                    for c in range(NCH):
                        ins = nc.tensor.matmul(b[0:CH, 0:GT], mean_w, src[:, c], start=(c == 0), stop=(c == NCH - 1))
                    ins.then_inc(projected, 1)
                elif kind == "gate":
                    pe.wait_ge(h1_s, 2 * g + 2)
                    pe.wait_ge(ld_ffn, 16 * 8)
                    b = take("g1", g)
                    for c in range(NCH):
                        ins = nc.tensor.matmul(by_image(b[0:32, 0:GT]), fg1_w[:, c], h1[0:CH, g, c, :, 0:TOK],
                                               start=(c == 0), stop=(c == NCH - 1))
                    ins.then_inc(projected, 1)
                elif kind == "fv":
                    for z in range(2):
                        b = take("fv", (g, z))
                        for jj in range(2):
                            j = 2 * z + jj
                            tile = lambda c, rows: h1[0:rows, g, c, 2 * j:2 * j + 2, :].rearrange("p i s -> p (i s)")
                            out = b[:, DIM * jj:DIM * jj + DIM]
                            nc.tensor.matmul(out, tile(0, CH + 1), fv_w[:, 0], start=True, stop=False)
                            ins = nc.tensor.matmul(out, tile(1, CH), fv_w[0:CH, 1], start=False, stop=True)
                        ins.then_inc(projected, 1)
                    b = take("lg", g)
                    pe.wait_ge(g1_s, 2 * g + 2)
                    for im in range(GI):
                        ins = nc.tensor.matmul(b[:, 3 * im:3 * im + 3], g1_t[:, im].rearrange("p d s -> p (d s)"),
                                               fg2_w[:], start=True, stop=True)
                    ins.then_inc(projected, 1)

            for i in range(ITERATIONS):
                if i - 1 in SEQ:
                    scores(SEQ[i - 1])
                if i - 2 in SEQ:
                    transposes(SEQ[i - 2])
                if i in SEQ:
                    project_qk(SEQ[i])
                if i - 2 in SEQ:
                    outputs(SEQ[i - 2])
                for s in STEPS.get(i, ()):
                    step(s)


def kernel(**inputs):
    import ml_dtypes
    import numpy as np
    import concourse.bacc as bacc
    from concourse.bass_utils import run_bass_kernel_spmd

    f = {k: np.asarray(v) for k, v in inputs.items()}
    x = f["x"].reshape(IMAGES, 3, 6, 16, 6, 16).transpose(1, 3, 5, 0, 2, 4).reshape(PK, 128, IMAGES * TOK)
    qkv = f["L0_attn_w_qkv"].reshape(NCH, CH, PAIRS, 2, 3, HD)
    chunks = lambda w: w.reshape(NCH, CH, -1).transpose(1, 0, 2)

    wqk, bqk = f["L0_ffn_Wqk"].reshape(DIM, 2, 3, HD), f["L0_ffn_bqk"].reshape(2, 3, HD)
    order = [(0, 0), (0, 1), (1, 0), (1, 1), (0, 2), (0, 2), (1, 2), (1, 2)]
    f_qk = np.concatenate([wqk[:, a, e] for a, e in order], axis=1)
    f_v = np.zeros((CH + 1, NCH, DIM), np.float32)
    f_v[0:CH] = chunks(f["L0_ffn_Wv"].transpose(1, 0, 2).reshape(DIM, DIM))
    f_v[CH, 0] = f["L0_ffn_bv"].reshape(DIM)

    biases = np.zeros((128, B_END), np.float32)
    for col, name in ((B_TOK, "L0_tok_bp"), (B_OUT, "L0_attn_b_out"), (B_FFN, "L0_ffn_bp")):
        biases[0:CH, col:col + NCH] = f[name].reshape(NCH, CH).T
    for n in range(4):
        biases[:, B_QK + n] = np.concatenate([bqk[order[2 * n]], bqk[order[2 * n + 1]]])
    biases[0:HD, B_CONVW:B_CONVW + 3] = f["L0_ffn_conv_w"].reshape(HD, 3)
    biases[0:HD, B_CONVB] = f["L0_ffn_conv_b"]
    biases[0:32, B_G1] = f["L0_ffn_bg1"]

    tok = np.arange(TOK)
    dist = tok[None, :] - tok[:, None]
    band, causal, outside = np.zeros((128, TOK)), np.zeros((128, TOK)), np.ones(128)
    for lo in (0, 64):
        band[lo:lo + TOK] = np.where(abs(dist) <= WINDOW_SIDE, 0.0, NEG)
        causal[lo:lo + TOK] = np.where(dist > 0, NEG, 0.0)
        outside[lo:lo + TOK] = 2 * WINDOW_SIDE + 1 - (abs(dist) <= WINDOW_SIDE).sum(1)
    consts = np.zeros((128, C_END), np.float32)
    consts[:, C_IDENT:C_IDENT + 128] = np.eye(128)
    consts[:, C_CAUSAL:C_CAUSAL + TOK] = causal
    consts[:, C_OUTSIDE] = outside
    consts[:, C_EPS] = 1e-5
    consts[:, C_MEAN:C_MEAN + CH] = 1.0 / DIM
    bf_consts = np.concatenate([np.eye(128), band, causal], axis=1).astype(ml_dtypes.bfloat16)

    arrays = {
        "x_t": x.transpose(1, 0, 2),
        "tok_w": f["L0_tok_Wp"].T.reshape(PK, 128, DIM).transpose(1, 0, 2),
        "w_qk": qkv[:, :, :, :, 0:2].transpose(1, 2, 0, 4, 3, 5).reshape(CH, PAIRS, NCH, 256),
        "w_v": qkv[:, :, :, :, 2].transpose(1, 0, 2, 3, 4).reshape(CH, NCH, PATCH),
        "w_out": f["L0_attn_w_out"].reshape(PAIRS, 128, DIM).transpose(1, 0, 2),
        "f_qk": chunks(f_qk), "f_v": f_v, "f_g1": chunks(f["L0_ffn_Wg1"]),
        "f_g2": np.concatenate([f["L0_ffn_Wg2"], f["L0_ffn_bg2"][None]]),
        "f_p01": f["L0_ffn_Wp"][0:128], "f_p2": f["L0_ffn_Wp"][128:DIM],
        "pos_bias": f["L0_ffn_pos_bias"][0:TOK, 0:TOK],
        "biases": biases, "consts": consts, "bf_consts": bf_consts,
    }
    arrays = {k: np.ascontiguousarray(a) for k, a in arrays.items()}
    nc = bacc.Bacc("TRN2", target_bir_lowering=False, num_devices=1)
    args = [nc.dram_tensor(k, a.shape, mybir.dt.from_np(a.dtype), kind="ExternalInput").ap() for k, a in arrays.items()]
    out = nc.dram_tensor("out_t", (CH, NCH, IMAGES * TOK), F32, kind="ExternalOutput").ap()
    vit_tower(nc, *args, out)
    got = run_bass_kernel_spmd(nc, [arrays], core_ids=[0]).results[0]["out_t"]
    return np.ascontiguousarray(got.transpose(2, 1, 0).reshape(IMAGES, TOK, DIM))
```

```python
from contextlib import ExitStack

import concourse.bass as bass
from concourse import mybir

F32 = mybir.dt.float32
F32R = mybir.dt.float32r
BF16 = mybir.dt.bfloat16
ALU = mybir.AluOpType
ACT = mybir.ActivationFunctionType
AX = mybir.AxisListType

IMAGES, TOK, SLOT = 16, 36, 64
GROUPS, GI = 2, 8
GT = GI * TOK
TILES = GI // 2
DIM, NCH = 192, 2
DUP = 256
PATCH, PK = 768, 6
PAIRS, HD = 6, 64
SCALE = 0.125
WINDOW_SIDE = 32
NEG = -1.0e30

C_IDENT, C_CAUSAL, C_OUTSIDE, C_EPS, C_MEAN = 0, 128, 164, 165, 166
C_END = C_MEAN + 128
B_TOK, B_OUT, B_FFN, B_QK, B_CONVW, B_CONVB, B_G1 = 0, 2, 4, 6, 10, 13, 14
B_END = 15

F_GATE = 512
F_VAL = F_GATE + 128
F_PROJ = F_VAL + DIM
F_END = F_PROJ + DUP
TOK_PIECES = [slice(0, 2), slice(2, 4), slice(4, 6)]
X_PIECES = [(0, ks) for ks in TOK_PIECES] + [(1, slice(0, 3)), (1, slice(3, 6))]

ATTN = [("attn", g, p) for g in range(GROUPS) for p in range(PAIRS)]
LINE = ATTN + [("ffn", 0, 0), ("ffn", 0, 1), None, None, None, ("ffn", 1, 0), ("ffn", 1, 1)]
QK_RING = 3
STEPS = {
    0: [("v", 0, 0), ("v", 0, 1)], 1: [("v", 0, 2), ("v", 0, 3)],
    4: [("v", 1, 0), ("v", 1, 1)], 5: [("v", 1, 2), ("v", 1, 3)],
    8: [("out", 0)], 9: [("mean", 0)], 10: [("var", 0)], 11: [("gate", 0), ("fv", 0)],
    14: [("out", 1)], 15: [("mean", 1)], 16: [("out2", 0), ("var", 1), ("mean2", 0)],
    17: [("gate", 1), ("fv", 1)], 18: [("var2", 0)], 21: [("out2", 1)], 22: [("mean2", 1)], 23: [("var2", 1)],
}
ITERATIONS = 24
SEQ = {}
for _i, _e in enumerate(LINE):
    if _e is not None:
        SEQ[_i] = len(SEQ)
ENTRY_OF = {LINE[_i]: _s for _i, _s in SEQ.items()}
entries = [LINE[_i] for _i in SEQ]


def vit_tower(nc, x_t, tok_w, w_qk, w_v, w_out, f_w, f_g2, f_bv, pos_bias, biases, consts, bf_consts, out_t):
    with ExitStack() as ctx:
        def sb(name, shape, dt=F32):
            return ctx.enter_context(nc.sbuf_tensor(name, shape, dt))

        def sem(name):
            return ctx.enter_context(nc.semaphore(name))

        x_f = sb("x_f", [128, GROUPS, PK, GT])
        x_hi = sb("x_hi", [128, GROUPS, PK, GT], F32R)
        x_lo = sb("x_lo", [128, GROUPS, PK, GT], F32R)
        tw_f = sb("tw_f", [128, PK, DUP])
        tw_hi = sb("tw_hi", [128, PK, DUP], F32R)
        tw_lo = sb("tw_lo", [128, PK, DUP], F32R)
        wqk_f = sb("wqk_f", [128, PAIRS, NCH, 256])
        wqk_hi = sb("wqk_hi", [128, PAIRS, NCH, 256], F32R)
        wqk_lo = sb("wqk_lo", [128, PAIRS, 256], F32R)
        wv_f = sb("wv_f", [128, NCH, PATCH])
        wv_hi = sb("wv_hi", [128, NCH, PATCH], F32R)
        wv_lo = sb("wv_lo", [128, PATCH], F32R)
        wo_f = sb("wo_f", [128, PAIRS, DUP])
        wo_hi = sb("wo_hi", [128, PAIRS, DUP], F32R)
        wo_lo = sb("wo_lo", [128, PAIRS, DUP], F32R)
        ffn_f = sb("ffn_f", [128, NCH, F_END])
        ffn_hi = sb("ffn_hi", [128, NCH, F_END], F32R)
        ffn_lo = sb("ffn_lo", [128, F_END], F32R)
        fg2_w = sb("fg2_w", [33, 3])
        bv_all = sb("bv_all", [128, DIM])
        bias = sb("bias", [128, B_END])
        const = sb("const", [128, C_END])
        bfc = sb("bfc", [128, 128 + 2 * TOK], BF16)
        posb = sb("posb", [128, TOK])
        posmask = sb("posmask", [128, TOK])
        ident = const[:, C_IDENT:C_IDENT + 128]
        outside = const[:, C_OUTSIDE:C_OUTSIDE + 1]
        eps = const[:, C_EPS:C_EPS + 1]
        mean_w = const[:, C_MEAN:C_MEAN + 128]
        ident_bf = bfc[:, 0:128]
        band_bf = bfc[:, 128:128 + TOK]
        causal_bf = bfc[:, 128 + TOK:128 + 2 * TOK]

        h_f = sb("h_f", [128, NCH, GROUPS, GT])
        h_hi = sb("h_hi", [128, NCH, IMAGES, SLOT], F32R)
        h_lo = sb("h_lo", [128, NCH, IMAGES, SLOT], F32R)
        n_seq = len(SEQ)
        q_t = sb("q_t", [128, QK_RING, GT])
        k_t = sb("k_t", [128, QK_RING, GT])
        qc_t = sb("qc_t", [HD, 2, GT])
        v_t = [sb("v_t", [128, TILES, PATCH])[:],
               x_f[:].rearrange("p g k t -> p (g k t)")[:, 0:TILES * PATCH].rearrange("p (j d) -> p j d", d=PATCH)]
        fv_t = wv_f[:].rearrange("p c (j d) -> p (c j) d", d=DIM)
        d_t = sb("d_t", [128, 2, GI, TOK])
        e_t = sb("e_t", [128, 2, GI, TOK])
        p_t = sb("p_t", [128, 2, GI, SLOT])
        pt_t = sb("pt_t", [128, 2, TILES, 2, 2, TOK])
        mx_t = sb("mx_t", [128, n_seq, 2, GI])
        z_t = sb("z_t", [128, n_seq, GI])
        sm_t = sb("sm_t", [128, n_seq, 3, GI])
        o_hi = x_hi
        o_lo = x_lo
        y_hi, y_lo = (t[:].rearrange("p k d -> p (k d)")[:, 0:GROUPS * 2 * GT].rearrange(
            "p (g c t) -> p g c t", g=GROUPS, c=2) for t in (tw_hi, tw_lo))
        r_t, c_t, sq_t, ln_t = (
            wqk_f[:].rearrange("p a c d -> p (a c d)")[:, n * NCH * GT:(n + 1) * NCH * GT].rearrange(
                "p (c t) -> p c t", c=NCH) for n in range(4))
        g1_t = sb("g1_t", [33, GI, 2, SLOT])
        n_ln, n_gm = 4 * NCH * GT, GROUPS * 8 * GI * 3
        gate_room = wqk_f[:].rearrange("p a c d -> p (a c d)")[:, n_ln:n_ln + n_gm + GROUPS * 8 * GI]
        gm = gate_room[:, 0:n_gm].rearrange("p (g z i e) -> p g z i e", g=GROUPS, z=8, e=3)
        gs = gate_room[:, n_gm:].rearrange("p (g z i) -> p g z i", g=GROUPS, z=8)
        wgt = sb("wgt", [128, GROUPS, 2, GI])
        out_s = tw_f[:].rearrange("p k d -> p (k d)")[:, 0:GROUPS * NCH * GT].rearrange(
            "p (g c t) -> p g c t", g=GROUPS, c=NCH)

        proj = [ctx.enter_context(nc.psum_tensor(f"proj{i}", [128, 512], F32)) for i in range(3)]
        score = [ctx.enter_context(nc.psum_tensor(f"score{i}", [128, 512], F32)) for i in range(2)]
        trans = ctx.enter_context(nc.psum_tensor("trans", [128, TILES, 2, SLOT], F32))
        outp = [ctx.enter_context(nc.psum_tensor(f"outp{i}", [128, 512], F32)) for i in range(2)]
        embed_bank = [[proj[0], proj[1]], [score[0], score[1]]]

        ld_const, ld_wv, ld_wo, ld_ffn, ld_small = (sem(s) for s in ("ld_const", "ld_wv", "ld_wo", "ld_ffn", "ld_small"))
        ld_x = [sem(f"ld_x{n}") for n in range(len(X_PIECES))]
        ld_tok = [sem(f"ld_tok{n}") for n in range(len(TOK_PIECES))]
        ld_qk = [sem(f"ld_qk{p}") for p in range(PAIRS // 2)]
        ld_bias = sem("ld_bias")
        st_out = sem("st_out")
        zeroed = sem("zeroed")
        tok_hi, tok_lo, x_hi_s, x_lo_s = (sem(s) for s in ("tok_hi", "tok_lo", "x_hi_s", "x_lo_s"))
        qk_hi, qk_lo, wv_hi_s, wv_lo_s, wo_hi_s, wo_lo_s = (
            sem(s) for s in ("qk_hi", "qk_lo", "wv_hi_s", "wv_lo_s", "wo_hi_s", "wo_lo_s"))
        posmask_s = sem("posmask_s")
        ffn_hi_s, ffn_lo_s, h1_hi_s, h1_lo_s = (sem(s) for s in ("ffn_hi_s", "ffn_lo_s", "h1_hi_s", "h1_lo_s"))
        embedded = sem("embedded")
        h_hi_s, h_f_s, h_lo_s = (sem(s) for s in ("h_hi_s", "h_f_s", "h_lo_s"))
        projected = sem("projected")
        scored = sem("scored")
        transposed = sem("transposed")
        attended = sem("attended")
        q_s, k_s = sem("q_s"), sem("k_s")
        v_s = sem("v_s")
        shifted, exped, zeroed_key, normed, pt_a, pt_d = (
            sem(s) for s in ("shifted", "exped", "outside_exped", "normed", "pt_a", "pt_d"))
        o_hi_s, o_lo_s = sem("o_hi_s"), sem("o_lo_s")
        res_s, cen_s, sq_s, rstd_s, h1_s = (sem(s) for s in ("res_s", "cen_s", "sq_s", "rstd_s", "h1_s"))
        g1_s, gate_exp, gate_exp2, gated, conv_s, fv_s = (
            sem(s) for s in ("g1_s", "gate_exp", "gate_exp2", "gated", "conv_s", "fv_s"))
        gate_d, gate_g, logit_s = sem("gate_d"), sem("gate_g"), sem("logit_s")
        outs = sem("outs")
        dve_chain, act_chain = sem("dve_chain"), sem("act_chain")

        uses, freed_by = {}, []

        def plan(kind, key, freed):
            uses[(kind, key)] = len(freed_by)
            freed_by.append(freed)

        n_res = n_stat = n_v = 0
        for i in range(ITERATIONS):
            if i in SEQ:
                plan("q", SEQ[i], (q_s, SEQ[i] + 1))
                plan("k", SEQ[i], (k_s, SEQ[i] + 1))
            for step in STEPS.get(i, ()):
                kind, g = step[0], step[1]
                if kind == "v":
                    n_v += 1
                    plan("v", (g, step[2], 0), (v_s, 2 * n_v - 1))
                    plan("v", (g, step[2], 1), (v_s, 2 * n_v))
                elif kind in ("out", "out2"):
                    for m in range(NCH):
                        n_res += 1
                        plan(kind, (g, m), (res_s, n_res))
                elif kind in ("mean", "mean2"):
                    plan(kind, g, (cen_s, len([u for u in uses if u[0] in ("mean", "mean2")]) + 1))
                elif kind in ("var", "var2"):
                    n_stat += 1
                    plan(kind, g, (act_chain, None))
                elif kind == "gate":
                    plan("g1", g, (g1_s, 2 * g + 2))
                elif kind == "fv":
                    plan("fv", (g, 0), (fv_s, 2 * g + 1))
                    plan("fv", (g, 1), (fv_s, 2 * g + 2))
                    plan("lg", g, (logit_s, g + 1))
        ln_order = [(s[0], s[1]) for i in range(ITERATIONS) for s in STEPS.get(i, ()) if s[0] in ("var", "var2")]
        ln_index = {s: n for n, s in enumerate(ln_order)}
        for (kind, key), n in list(uses.items()):
            if kind in ("var", "var2"):
                freed_by[n] = (rstd_s, ln_index[(kind, key)] + 1)
        norm_of = {("out", 0): ("var", 0), ("out", 1): ("var", 1), ("out2", 0): ("var2", 0), ("out2", 1): ("var2", 1)}

        def bank(kind, key):
            return proj[uses[(kind, key)] % 3]

        def hcols(t, g, c, rows=128):
            return t[0:rows, c, GI * g:GI * g + GI, 0:TOK]

        def by_image(ap):
            return ap.rearrange("p (i t) -> p i t", t=TOK)

        ZEROED = 6
        block = ctx.enter_context(nc.Block())

        @block.sync
        def _(sp):
            for n, ks in enumerate(TOK_PIECES):
                sp.dma_start(tw_f[:, ks], tok_w[:, ks]).then_inc(ld_tok[n], 16)
                sp.dma_start(x_f[:, 0, ks], x_t[:, 0, ks]).then_inc(ld_x[n], 16)
            for n, (g, ks) in enumerate(X_PIECES):
                if g:
                    sp.dma_start(x_f[:, g, ks], x_t[:, g, ks]).then_inc(ld_x[n], 16)
            sp.dma_start(bias[:], biases).then_inc(ld_bias, 16)
            for n in range(PAIRS // 2):
                sp.dma_start(wqk_f[:, 2 * n:2 * n + 2], w_qk[:, 2 * n:2 * n + 2]).then_inc(ld_qk[n], 16)
                if n == 0:
                    sp.dma_start(wv_f[:], w_v).then_inc(ld_wv, 16)
                    sp.dma_start(bfc[:], bf_consts).then_inc(ld_const, 16)
                    sp.dma_start(const[:], consts).then_inc(ld_const, 16)
            sp.dma_start(wo_f[:], w_out).then_inc(ld_wo, 16)
            sp.dma_start(ffn_f[:], f_w).then_inc(ld_ffn, 16)
            sp.dma_start(fg2_w[:], f_g2).then_inc(ld_small, 16)
            sp.dma_start(bv_all[:], f_bv).then_inc(ld_small, 16)
            sp.dma_start(posb[:], pos_bias).then_inc(ld_small, 16)
            for n, g in enumerate((0, 1)):
                sp.wait_ge(outs, n + 1)
                cols = slice(g * GT, (g + 1) * GT)
                sp.dma_start(out_t[0:128, cols], out_s[:, g, 0]).then_inc(st_out, 16)
                sp.dma_start(out_t[128:DIM, cols], out_s[0:64, g, 1]).then_inc(st_out, 16)
            sp.wait_ge(st_out, 32 * GROUPS)

        @block.gpsimd
        def _(pool):
            for t in (h_hi, h_lo, p_t, pt_t, g1_t):
                pool.memset(t[:].bitcast(F32), 0.0).then_inc(zeroed, 1)
            pool.wait_ge(zeroed, 5)
            pool.memset(g1_t[32:33], 1.0).then_inc(zeroed, 1)
            pool.wait_ge(zeroed, 6)

            def lo_part(lo, hi, raw, done, before):
                nc.gpsimd.tensor_tensor(lo, raw[:, 0], hi[:, 0].bitcast(F32), ALU.subtract).then_inc(done, 1)
                pool.wait_ge(done, before + 1)
                nc.gpsimd.tensor_tensor(hi[64:128, 1], raw[64:128, 1], hi[64:128, 1].bitcast(F32),
                                        ALU.subtract).then_inc(done, 1)
                pool.wait_ge(done, before + 2)

            for p in range(PAIRS):
                pool.wait_ge(qk_hi, p // 2 + 1)
                lo_part(wqk_lo[:, p], wqk_hi[:, p], wqk_f[:, p], qk_lo, 2 * p)
            pool.wait_ge(wo_hi_s, 1)
            nc.gpsimd.tensor_tensor(wo_lo[:], wo_f[:], wo_hi[:].bitcast(F32), ALU.subtract).then_inc(wo_lo_s, 1)
            pool.wait_ge(wo_lo_s, 1)
            pool.wait_ge(ffn_hi_s, 1)
            lo_part(ffn_lo[:], ffn_hi[:], ffn_f[:], ffn_lo_s, 0)

        @block.scalar
        def _(act):
            act.preload_act_table_set("natural_log_exp_and_others")
            for n, (g, ks) in enumerate(X_PIECES):
                if g == 0:
                    act.wait_ge(ld_tok[n], 16)
                    nc.scalar.activation(tw_hi[:, ks], tw_f[:, ks], ACT.Copy).then_inc(tok_hi, 1)
                act.wait_ge(ld_x[n], 16)
                nc.scalar.activation(x_hi[:, g, ks], x_f[:, g, ks], ACT.Copy).then_inc(x_hi_s, 1)

            def raw_hi(n):
                act.wait_ge(ld_qk[n], 16)
                nc.scalar.activation(wqk_hi[:, 2 * n:2 * n + 2], wqk_f[:, 2 * n:2 * n + 2],
                                     ACT.Copy).then_inc(qk_hi, 1)

            raw_hi(0)
            act.wait_ge(ld_wv, 16)
            nc.scalar.activation(wv_hi[:], wv_f[:], ACT.Copy).then_inc(wv_hi_s, 1)
            act.wait_ge(ld_bias, 16)
            act.wait_ge(zeroed, ZEROED)
            for n, (g, m) in enumerate((g, m) for g in range(GROUPS) for m in range(NCH)):
                act.wait_ge(embedded, n + 1)
                nc.scalar.activation(hcols(h_hi, g, m), by_image(embed_bank[g][m][:, 0:GT]), ACT.Identity,
                                     bias=bias[:, B_TOK + m:B_TOK + m + 1]).then_inc(h_hi_s, 1)

            def copy_q_k(n):
                kind, g, p = entries[n]
                if n >= QK_RING:
                    act.wait_ge(scored, n - QK_RING + 1)
                for which, (dst, name, done) in enumerate(((q_t, "q", q_s), (k_t, "k", k_s))):
                    act.wait_ge(projected, uses[(name, n)] + 1)
                    b = bank(name, n)[:, 0:GT]
                    if kind == "attn":
                        nc.scalar.activation(dst[:, n % QK_RING], b, ACT.Copy).then_inc(done, 1)
                    else:
                        col = B_QK + 2 * p + which
                        nc.scalar.activation(dst[:, n % QK_RING], b, ACT.Identity, bias=bias[:, col:col + 1]).then_inc(done, 1)

            def exp_scores(n):
                if n >= 2:
                    act.wait_ge(normed, n - 1)
                act.wait_ge(shifted, n + 1)
                nc.scalar.activation(e_t[:, n % 2], d_t[:, n % 2], ACT.Exp, scale=SCALE).then_inc(exped, 1)
                if entries[n][0] == "attn":
                    nc.scalar.activation(z_t[:, n], mx_t[:, n, 1], ACT.Exp, scale=-SCALE).then_inc(zeroed_key, 1)

            def copy_transposed(n):
                act.wait_ge(transposed, n + 1)
                if n >= 2:
                    act.wait_ge(attended, n - 1)
                nc.scalar.activation(pt_t[0:64, n % 2, :, :, 0], trans[0:64, :, :, 0:TOK], ACT.Copy).then_inc(pt_a, 1)

            def copy_outputs(n):
                kind, g, p = entries[n]
                act.wait_ge(attended, n + 1)
                dst = o_hi[:, g, p] if kind == "attn" else y_hi[:, g, p]
                nc.scalar.activation(dst, outp[n % 2][:, 0:GT], ACT.Copy).then_inc(o_hi_s, 1)

            def step(s):
                kind, g = s[0], s[1]
                if kind == "v":
                    for half in range(2):
                        u = (g, s[2], half)
                        act.wait_ge(projected, uses[("v", u)] + 1)
                        nc.scalar.activation(v_t[g][:, s[2], 384 * half:384 * half + 384], bank("v", u)[:, 0:384],
                                             ACT.Copy).then_inc(v_s, 1)
                elif kind in ("mean", "mean2"):
                    n = ln_index[(kind.replace("mean", "var"), g)]
                    act.wait_ge(cen_s, n + 1)
                    nc.scalar.activation(sq_t, c_t, ACT.Square).then_inc(sq_s, 1)
                elif kind in ("var", "var2"):
                    n = ln_index[(kind, g)]
                    act.wait_ge(projected, uses[(kind, g)] + 1)
                    nc.scalar.activation(ln_t[:, 0], bank(kind, g)[:, 0:GT], ACT.Ln, bias=eps).then_inc(act_chain, 1)
                    act.wait_ge(act_chain, n + 1)
                    nc.scalar.activation(ln_t[:, 1], ln_t[:, 0], ACT.Exp, scale=-0.5).then_inc(rstd_s, 1)
                    if kind == "var":
                        act.wait_ge(h1_s, g + 1)
                        nc.scalar.activation(h_hi[:, :, GI * g:GI * g + GI, 0:TOK].rearrange("p c i t -> p c i t"),
                                             h_f[:, :, g].rearrange("p c (i t) -> p c i t", t=TOK),
                                             ACT.Copy).then_inc(h1_hi_s, 1)
                elif kind == "gate":
                    act.wait_ge(projected, uses[("g1", g)] + 1)
                    src = by_image(bank("g1", g)[0:32, 0:GT])
                    if g:
                        act.wait_ge(logit_s, g)
                    for dup in range(2):
                        nc.scalar.activation(g1_t[0:32, :, dup, 0:TOK], src, ACT.Relu,
                                             bias=bias[0:32, B_G1:B_G1 + 1]).then_inc(g1_s, 1)
                elif kind == "fv":
                    act.wait_ge(gate_d, g + 1)
                    nc.scalar.activation(gm[:, g, 1], gm[:, g, 0], ACT.Exp).then_inc(gate_exp, 1)
                    act.wait_ge(gate_g, g + 1)
                    nc.scalar.activation(gm[:, g, 4], gm[:, g, 3], ACT.Exp).then_inc(gate_exp2, 1)

            for i in range(ITERATIONS):
                if i in SEQ:
                    copy_q_k(SEQ[i])
                if i - 3 in SEQ:
                    copy_outputs(SEQ[i - 3])
                if i - 2 in SEQ:
                    copy_transposed(SEQ[i - 2])
                if i - 1 in SEQ:
                    exp_scores(SEQ[i - 1])
                if i < 2:
                    raw_hi(i + 1)
                if i == 2:
                    act.wait_ge(ld_wo, 16)
                    nc.scalar.activation(wo_hi[:], wo_f[:], ACT.Copy).then_inc(wo_hi_s, 1)
                if i == 3:
                    act.wait_ge(ld_ffn, 16)
                    nc.scalar.activation(ffn_hi[:], ffn_f[:], ACT.Copy).then_inc(ffn_hi_s, 1)
                for s in STEPS.get(i, ()):
                    step(s)

        @block.vector
        def _(dve):
            chain = [0]

            def link(ins):
                chain[0] += 1
                ins.then_inc(dve_chain, 1)
                dve.wait_ge(dve_chain, chain[0])

            for n, (g, ks) in enumerate(X_PIECES):
                if g == 0:
                    dve.wait_ge(tok_hi, n + 1)
                    nc.vector.tensor_tensor(tw_lo[:, ks], tw_f[:, ks], tw_hi[:, ks].bitcast(F32),
                                            ALU.subtract).then_inc(tok_lo, 1)
                dve.wait_ge(x_hi_s, n + 1)
                nc.vector.tensor_tensor(x_lo[:, g, ks], x_f[:, g, ks], x_hi[:, g, ks].bitcast(F32),
                                        ALU.subtract).then_inc(x_lo_s, 1)
            dve.wait_ge(wv_hi_s, 1)
            nc.vector.tensor_tensor(wv_lo[:], wv_f[:, 0], wv_hi[:, 0].bitcast(F32), ALU.subtract).then_inc(wv_lo_s, 1)
            nc.vector.tensor_tensor(wv_hi[64:128, 1], wv_f[64:128, 1], wv_hi[64:128, 1].bitcast(F32),
                                    ALU.subtract).then_inc(wv_lo_s, 1)
            dve.wait_ge(ld_bias, 16)
            dve.wait_ge(zeroed, ZEROED)
            for n, (g, m) in enumerate((g, m) for g in range(GROUPS) for m in range(NCH)):
                dve.wait_ge(h_hi_s, n + 1)
                nc.vector.tensor_scalar(h_f[:, m, g], embed_bank[g][m][:, 0:GT],
                                        bias[:, B_TOK + m:B_TOK + m + 1], None, ALU.add).then_inc(h_f_s, 1)
                dve.wait_ge(h_f_s, n + 1)
                nc.vector.tensor_tensor(hcols(h_lo, g, m), by_image(h_f[:, m, g]), hcols(h_hi, g, m).bitcast(F32),
                                        ALU.subtract).then_inc(h_lo_s, 1)
            dve.wait_ge(ld_small, 16 * 3)
            dve.wait_ge(ld_const, 32)
            nc.vector.scalar_tensor_tensor(out=posmask[:], in0=posb[:], scalar=1.0 / SCALE,
                                           in1=const[:, C_CAUSAL:C_CAUSAL + TOK], op0=ALU.mult,
                                           op1=ALU.add).then_inc(posmask_s, 1)

            def shift_scores(n):
                kind, g, p = entries[n]
                s = by_image(score[n % 2][:, 0:GT])
                dve.wait_ge(scored, n + 1)
                if kind == "attn":
                    link(nc.vector.tensor_reduce(mx_t[:, n, 0], s, AX.X, ALU.max))
                    link(nc.vector.tensor_scalar(mx_t[:, n, 1], mx_t[:, n, 0], 0.0, None, ALU.max))
                else:
                    link(nc.vector.tensor_reduce(mx_t[:, n, 1], s, AX.X, ALU.max))
                if n >= 2:
                    dve.wait_ge(exped, n - 1)
                nc.vector.tensor_tensor(d_t[:, n % 2], s, mx_t[:, n, 1].unsqueeze(2).broadcast_to([128, GI, TOK]),
                                        ALU.subtract).then_inc(shifted, 1)

            def normalise(n):
                kind, g, p = entries[n]
                dve.wait_ge(exped, n + 1)
                link(nc.vector.tensor_reduce(sm_t[:, n, 0], e_t[:, n % 2], AX.X, ALU.add))
                if kind == "attn":
                    dve.wait_ge(zeroed_key, n + 1 if n < 12 else 12)
                    link(nc.vector.scalar_tensor_tensor(out=sm_t[:, n, 1], in0=z_t[:, n], scalar=outside,
                                                        in1=sm_t[:, n, 0], op0=ALU.mult, op1=ALU.add))
                    link(nc.vector.reciprocal(sm_t[:, n, 2], sm_t[:, n, 1]))
                else:
                    link(nc.vector.reciprocal(sm_t[:, n, 1], sm_t[:, n, 0]))
                    dve.wait_ge(gated, 3 * g + 3)
                    link(nc.vector.tensor_tensor(sm_t[:, n, 2], sm_t[:, n, 1], wgt[:, g, p], ALU.mult))
                if n >= 2:
                    dve.wait_ge(transposed, n - 1)
                nc.vector.tensor_tensor(p_t[:, n % 2, :, 0:TOK], e_t[:, n % 2],
                                        sm_t[:, n, 2].unsqueeze(2).broadcast_to([128, GI, TOK]),
                                        ALU.mult).then_inc(normed, 1)

            def copy_transposed(n):
                dve.wait_ge(transposed, n + 1)
                if n >= 2:
                    dve.wait_ge(attended, n - 1)
                nc.vector.tensor_copy(pt_t[64:128, n % 2, :, :, 1], trans[64:128, :, :, 0:TOK]).then_inc(pt_d, 1)

            def outputs_lo(n):
                kind, g, p = entries[n]
                dve.wait_ge(o_hi_s, n + 1)
                hi, lo = (o_hi[:, g, p], o_lo[:, g, p]) if kind == "attn" else (y_hi[:, g, p], y_lo[:, g, p])
                nc.vector.tensor_tensor(lo, outp[n % 2][:, 0:GT], hi.bitcast(F32), ALU.subtract).then_inc(o_lo_s, 1)

            def convolve(n):
                g = entries[n][1]
                dve.wait_ge(q_s, n + 1)
                if g:
                    dve.wait_ge(scored, n)
                q = by_image(q_t[0:HD, n % QK_RING])
                a, b = (by_image(qc_t[:, z]) for z in range(2))
                w = [bias[0:HD, B_CONVW + j:B_CONVW + j + 1] for j in range(3)]
                link(nc.vector.tensor_scalar(a, q, w[1], bias[0:HD, B_CONVB:B_CONVB + 1], ALU.mult, ALU.add))
                nc.vector.tensor_copy(b[:, :, 0:1], a[:, :, 0:1])
                link(nc.vector.scalar_tensor_tensor(out=b[:, :, 1:TOK], in0=q[:, :, 0:TOK - 1], scalar=w[0],
                                                    in1=a[:, :, 1:TOK], op0=ALU.mult, op1=ALU.add))
                link(nc.vector.tensor_copy(a[:, :, TOK - 1:TOK], b[:, :, TOK - 1:TOK]))
                nc.vector.scalar_tensor_tensor(out=a[:, :, 0:TOK - 1], in0=q[:, :, 1:TOK], scalar=w[2],
                                               in1=b[:, :, 0:TOK - 1], op0=ALU.mult, op1=ALU.add).then_inc(conv_s, 1)

            def gate(g):
                t = [gm[:, g, z] for z in range(8)]
                s = [gs[:, g, z] for z in range(8)]
                wide = lambda z: z.unsqueeze(2).broadcast_to([128, GI, 3])
                dve.wait_ge(projected, uses[("lg", g)] + 1)
                lg = bank("lg", g)[:, 0:3 * GI].rearrange("p (i e) -> p i e", e=3)
                link(nc.vector.tensor_reduce(s[0], lg, AX.X, ALU.max))
                link(nc.vector.tensor_tensor(t[0], lg, wide(s[0]), ALU.subtract))
                dve.sem_inc(gate_d, 1)
                dve.sem_inc(logit_s, 1)
                dve.wait_ge(gate_exp, g + 1)
                link(nc.vector.tensor_reduce(s[1], t[1], AX.X, ALU.add))
                link(nc.vector.reciprocal(s[2], s[1]))
                link(nc.vector.tensor_tensor(t[2], t[1], wide(s[2]), ALU.mult))
                link(nc.vector.tensor_reduce(s[3], t[2], AX.X, ALU.max))
                nc.vector.tensor_tensor(t[3], t[2], wide(s[3]), ALU.subtract).then_inc(gate_g, 1)
                g0, g1, g2 = (t[2][:, :, z] for z in range(3))
                nc.vector.tensor_tensor(s[4], g0, g1, ALU.min)
                link(nc.vector.tensor_tensor(s[5], g1, g2, ALU.min))
                keep = t[5]
                nc.vector.tensor_tensor(keep[:, :, 2], g2, s[4], ALU.is_gt)
                link(nc.vector.tensor_tensor(keep[:, :, 0], g0, s[5], ALU.is_ge))
                link(nc.vector.tensor_tensor(s[6], keep[:, :, 0], keep[:, :, 2], ALU.add))
                link(nc.vector.tensor_scalar(keep[:, :, 1], s[6], -1.0, 2.0, ALU.mult, ALU.add))
                dve.wait_ge(gate_exp2, g + 1)
                link(nc.vector.tensor_tensor(t[6], t[4], keep, ALU.mult))
                link(nc.vector.tensor_reduce(s[7], t[6], AX.X, ALU.add))
                link(nc.vector.reciprocal(s[0], s[7]))
                link(nc.vector.tensor_tensor(t[7], t[6], wide(s[0]), ALU.mult))
                nc.vector.tensor_copy(wgt[0:64, g, 0], t[7][0:64, :, 0]).then_inc(gated, 1)
                nc.vector.tensor_copy(wgt[64:128, g, 0], t[7][64:128, :, 1]).then_inc(gated, 1)
                nc.vector.tensor_copy(wgt[:, g, 1], t[7][:, :, 2]).then_inc(gated, 1)

            def step(s):
                kind, g = s[0], s[1]
                if kind in ("out", "out2"):
                    n = ln_index[norm_of[(kind, g)]]
                    if n:
                        dve.wait_ge(cen_s, n)
                    for m in range(NCH):
                        dve.wait_ge(projected, uses[(kind, (g, m))] + 1)
                        col = (B_OUT if kind == "out" else B_FFN) + m
                        nc.vector.scalar_tensor_tensor(out=r_t[:, m], in0=bank(kind, (g, m))[:, 0:GT],
                                                       scalar=bias[:, col:col + 1], in1=h_f[:, m, g], op0=ALU.add,
                                                       op1=ALU.add).then_inc(res_s, 1)
                elif kind in ("mean", "mean2"):
                    n = ln_index[(kind.replace("mean", "var"), g)]
                    dve.wait_ge(projected, uses[(kind, g)] + 1)
                    if n:
                        dve.wait_ge(sq_s, n)
                    nc.vector.tensor_tensor(c_t, r_t[:], bank(kind, g)[:, 0:GT].unsqueeze(1)
                                            .broadcast_to([128, NCH, GT]), ALU.subtract).then_inc(cen_s, 1)
                elif kind in ("var", "var2"):
                    n = ln_index[(kind, g)]
                    dve.wait_ge(rstd_s, n + 1)
                    dst = h_f[:, :, g] if kind == "var" else out_s[:, g]
                    nc.vector.tensor_tensor(dst, c_t, ln_t[:, 1].unsqueeze(1).broadcast_to([128, NCH, GT]),
                                            ALU.mult).then_inc(h1_s if kind == "var" else outs, 1)
                    if kind == "var":
                        dve.wait_ge(h1_hi_s, g + 1)
                        nc.vector.tensor_tensor(h_lo[:, :, GI * g:GI * g + GI, 0:TOK],
                                                h_f[:, :, g].rearrange("p c (i t) -> p c i t", t=TOK),
                                                h_hi[:, :, GI * g:GI * g + GI, 0:TOK].bitcast(F32),
                                                ALU.subtract).then_inc(h1_lo_s, 1)
                elif kind == "fv":
                    for z in range(2):
                        dve.wait_ge(projected, uses[("fv", (g, z))] + 1)
                        src = bank("fv", (g, z))[:, 0:2 * DIM].rearrange("p (j d) -> p j d", d=DIM)
                        nc.vector.tensor_tensor(fv_t[:, TILES * g + 2 * z:TILES * g + 2 * z + 2], src,
                                                bv_all[:].unsqueeze(1).broadcast_to([128, 2, DIM]),
                                                ALU.add).then_inc(fv_s, 1)
                    gate(g)

            for i in range(ITERATIONS):
                if i in SEQ and LINE[i][0] == "ffn" and LINE[i][2] == 0:
                    convolve(SEQ[i])
                if i - 3 in SEQ:
                    outputs_lo(SEQ[i - 3])
                if i - 1 in SEQ:
                    shift_scores(SEQ[i - 1])
                if i - 2 in SEQ:
                    copy_transposed(SEQ[i - 2])
                if i - 1 in SEQ:
                    normalise(SEQ[i - 1])
                for s in STEPS.get(i, ()):
                    step(s)

        @block.tensor
        def _(pe):
            def features(out, w_hi, w_lo, h, tokens_first=False):
                ops = [(w_hi[:, 0], h(h_hi, 0, 128)), (w_hi[:, 0], h(h_lo, 0, 128)), (w_lo, h(h_hi, 0, 128)),
                       (w_hi[:, 1], h(h_hi, 1, 128)), (w_hi[0:64, 1], h(h_lo, 1, 64))]
                for n, (a, b) in enumerate(ops):
                    if tokens_first:
                        a, b = b, a
                    ins = nc.tensor.matmul(out, a, b, start=(n == 0), stop=(n == len(ops) - 1))
                return ins

            def take(kind, key):
                n = uses[(kind, key)]
                if n >= 3:
                    pe.wait_ge(*freed_by[n - 3])
                return proj[n % 3]

            for n, (g, ks) in enumerate(X_PIECES):
                pe.wait_ge(x_lo_s, n + 1)
                if g == 0:
                    pe.wait_ge(tok_lo, n + 1)
                for k in range(ks.start, ks.stop):
                    for m in range(NCH):
                        cols = slice(128 * m, 128 * m + 128)
                        for z, (a, b) in enumerate(((tw_hi, x_hi), (tw_hi, x_lo), (tw_lo, x_hi))):
                            ins = nc.tensor.matmul(embed_bank[g][m][:, 0:GT], a[:, k, cols], b[:, g, k],
                                                   start=(k == 0 and z == 0), stop=(k == PK - 1 and z == 2))
                        if k == PK - 1:
                            ins.then_inc(embedded, 1)
            pe.wait_ge(zeroed, ZEROED)

            def project_qk(n):
                kind, g, p = entries[n]
                if kind == "attn":
                    pe.wait_ge(qk_lo, 2 * p + 2)
                    pe.wait_ge(h_lo_s, NCH * g + NCH)
                    pe.wait_ge(h_hi_s, NCH * g + NCH)
                    w_hi, w_lo = wqk_hi[:, p], wqk_lo[:, p]
                else:
                    pe.wait_ge(h1_lo_s, g + 1)
                    pe.wait_ge(ffn_lo_s, 2)
                    w_hi, w_lo = (w[..., 256 * p:256 * p + 256] for w in (ffn_hi, ffn_lo))
                for which, name in enumerate("qk"):
                    b = take(name, n)
                    cols = slice(128 * which, 128 * which + 128)
                    features(by_image(b[:, 0:GT]), w_hi[:, :, cols], w_lo[:, cols],
                             lambda t, c, rows: hcols(t, g, c, rows)).then_inc(projected, 1)

            def scores(n):
                kind, g, p = entries[n]
                out = by_image(score[n % 2][:, 0:GT])
                pe.wait_ge(k_s, n + 1)
                pe.wait_ge(q_s, n + 1)
                if n == 0:
                    pe.wait_ge(h_lo_s, NCH * GROUPS)
                    pe.wait_ge(ld_const, 32)
                if n >= 2:
                    pe.wait_ge(shifted, n - 1)
                if (kind, p) == ("ffn", 0):
                    pe.wait_ge(conv_s, g + 1)
                if (kind, p) == ("ffn", 1):
                    pe.wait_ge(posmask_s, 1)
                    idn, mask = ident, posmask[:]
                else:
                    idn, mask = ident_bf, band_bf if kind == "attn" else causal_bf
                nc.tensor.matmul(out, idn, mask.unsqueeze(1).broadcast_to([128, GI, TOK]), start=True, stop=False,
                                 skip_group_check=True)
                for im in range(GI):
                    cols = slice(TOK * im, TOK * im + TOK)
                    for h in range(2):
                        rows = slice(HD * h, HD * h + HD)
                        q = qc_t[:, 0, cols] if (kind, p, h) == ("ffn", 0, 0) else q_t[rows, n % QK_RING, cols]
                        ins = nc.tensor.matmul(score[n % 2][64 * h:64 * h + TOK, cols], q, k_t[rows, n % QK_RING, cols],
                                               start=False, stop=True, skip_group_check=True)
                ins.then_inc(scored, 1)

            def transposes(n):
                pe.wait_ge(normed, n + 1)
                if n >= 1:
                    pe.wait_ge(pt_a, n)
                    pe.wait_ge(pt_d, n)
                for j in range(TILES):
                    src = p_t[:, n % 2, 2 * j:2 * j + 2, :].rearrange("p i s -> p (i s)")
                    ins = nc.tensor.transpose(trans[:, j].rearrange("p h s -> p (h s)"), src, ident)
                ins.then_inc(transposed, 1)

            def outputs(n):
                kind, g, p = entries[n]
                pe.wait_ge(pt_a, n + 1)
                pe.wait_ge(pt_d, n + 1)
                if n >= 2:
                    pe.wait_ge(o_lo_s, n - 1)
                if kind == "attn":
                    pe.wait_ge(v_s, 2 * TILES * (g + 1))
                else:
                    pe.wait_ge(fv_s, 2 * g + 2)
                val = v_t[g] if kind == "attn" else fv_t[:, TILES * g:TILES * g + TILES]
                for j in range(TILES):
                    for h in range(2):
                        d = HD * (2 * p + h) if (kind, p) != ("ffn", 1) else 2 * HD
                        ins = nc.tensor.matmul(outp[n % 2][HD * h:HD * h + HD, 2 * TOK * j:2 * TOK * (j + 1)],
                                               val[:, j, d:d + HD], pt_t[:, n % 2, j, h].rearrange("p i t -> p (i t)"),
                                               start=True, stop=True)
                ins.then_inc(attended, 1)

            def step(s):
                kind, g = s[0], s[1]
                if kind == "v":
                    pe.wait_ge(wv_lo_s, 2)
                    for half in range(2):
                        b = take("v", (g, s[2], half))
                        im, cols = GI * g + 2 * s[2], slice(384 * half, 384 * half + 384)
                        features(b[:, 0:384], wv_hi[:, :, cols], wv_lo[:, cols],
                                 lambda t, c, rows: t[0:rows, c, im:im + 2, :].rearrange("p i s -> p (i s)"),
                                 tokens_first=True).then_inc(projected, 1)
                elif kind == "out":
                    pe.wait_ge(wo_lo_s, 1)
                    for m in range(NCH):
                        b = take("out", (g, m))
                        cols = slice(128 * m, 128 * m + 128)
                        for p in range(PAIRS):
                            pe.wait_ge(o_lo_s, ENTRY_OF[("attn", g, p)] + 1)
                            for z, (w, o) in enumerate(((wo_hi, o_hi), (wo_hi, o_lo), (wo_lo, o_hi))):
                                ins = nc.tensor.matmul(b[:, 0:GT], w[:, p, cols], o[:, g, p],
                                                       start=(p == 0 and z == 0), stop=(p == PAIRS - 1 and z == 2))
                        ins.then_inc(projected, 1)
                elif kind == "out2":
                    pe.wait_ge(o_lo_s, ENTRY_OF[("ffn", g, 1)] + 1)
                    for m in range(NCH):
                        b = take("out2", (g, m))
                        cols = slice(F_PROJ + 128 * m, F_PROJ + 128 * m + 128)
                        ops = [(ffn_hi[:, 0, cols], y_hi[:, g, 0]), (ffn_hi[:, 0, cols], y_lo[:, g, 0]),
                               (ffn_lo[:, cols], y_hi[:, g, 0]), (ffn_hi[:, 1, cols], y_hi[:, g, 1]),
                               (ffn_hi[0:64, 1, cols], y_lo[0:64, g, 1])]
                        for z, (w, y) in enumerate(ops):
                            ins = nc.tensor.matmul(b[:, 0:GT], w, y, start=(z == 0), stop=(z == 4))
                        ins.then_inc(projected, 1)
                elif kind in ("mean", "mean2", "var", "var2"):
                    n = ln_index[(kind.replace("mean", "var"), g)]
                    if kind.startswith("mean"):
                        pe.wait_ge(res_s, 2 * n + 2)
                        src = r_t
                    else:
                        pe.wait_ge(sq_s, n + 1)
                        src = sq_t
                    pe.wait_ge(ld_const, 32)
                    b = take(kind, g)
                    nc.tensor.matmul(b[:, 0:GT], mean_w, src[:, 0], start=True, stop=False)
                    nc.tensor.matmul(b[:, 0:GT], mean_w[0:64], src[0:64, 1], start=False, stop=True
                                     ).then_inc(projected, 1)
                elif kind == "gate":
                    pe.wait_ge(h1_lo_s, g + 1)
                    pe.wait_ge(ffn_lo_s, 2)
                    b = take("g1", g)
                    cols = slice(F_GATE, F_GATE + 128)
                    features(by_image(b[:, 0:GT]), ffn_hi[:, :, cols], ffn_lo[:, cols],
                             lambda t, c, rows: hcols(t, g, c, rows)).then_inc(projected, 1)
                elif kind == "fv":
                    cols = slice(F_VAL, F_VAL + DIM)
                    for z in range(2):
                        b = take("fv", (g, z))
                        for jj in range(2):
                            im = GI * g + 4 * z + 2 * jj
                            ins = features(b[:, DIM * jj:DIM * jj + DIM], ffn_hi[:, :, cols], ffn_lo[:, cols],
                                           lambda t, c, rows: t[0:rows, c, im:im + 2, :].rearrange("p i s -> p (i s)"),
                                           tokens_first=True)
                        ins.then_inc(projected, 1)
                    b = take("lg", g)
                    pe.wait_ge(ld_small, 16 * 3)
                    pe.wait_ge(g1_s, 2 * g + 2)
                    for im in range(GI):
                        ins = nc.tensor.matmul(b[:, 3 * im:3 * im + 3], g1_t[:, im].rearrange("p d s -> p (d s)"),
                                               fg2_w[:], start=True, stop=True)
                    ins.then_inc(projected, 1)

            for i in range(ITERATIONS):
                if i in SEQ:
                    project_qk(SEQ[i])
                if i - 3 in SEQ:
                    outputs(SEQ[i - 3])
                if i - 1 in SEQ:
                    scores(SEQ[i - 1])
                if i - 2 in SEQ:
                    transposes(SEQ[i - 2])
                for s in STEPS.get(i, ()):
                    step(s)


def kernel(**inputs):
    import ml_dtypes
    import numpy as np
    import concourse.bacc as bacc
    from concourse.bass_utils import run_bass_kernel_spmd

    f = {k: np.asarray(v) for k, v in inputs.items()}
    twice = lambda w: np.concatenate([w, w[..., 128:DIM]], axis=-1)
    chunks = lambda w: np.stack([w[0:128], np.concatenate([w[128:DIM]] * 2)], axis=1)
    x = f["x"].reshape(GROUPS, GI, 3, 6, 16, 6, 16).transpose(2, 4, 6, 0, 1, 3, 5)
    x = x.reshape(PK, 128, GROUPS, GT).transpose(1, 2, 0, 3)
    qkv = f["L0_attn_w_qkv"].reshape(DIM, PAIRS, 2, 3, HD)
    w_qk = chunks(qkv[:, :, :, 0:2].transpose(0, 1, 3, 2, 4).reshape(DIM, PAIRS, 256)).transpose(0, 2, 1, 3)

    wqk, bqk = f["L0_ffn_Wqk"].reshape(DIM, 2, 3, HD), f["L0_ffn_bqk"].reshape(2, 3, HD)
    order = [(0, 0), (0, 1), (1, 0), (1, 1), (0, 2), (0, 2), (1, 2), (1, 2)]
    f_w = np.concatenate([wqk[:, a, e] for a, e in order] + [f["L0_ffn_Wg1"], np.zeros((DIM, 96), np.float32)]
                         + list(f["L0_ffn_Wv"]) + [twice(f["L0_ffn_Wp"])], axis=1)

    biases = np.zeros((128, B_END), np.float32)
    for col, name in ((B_TOK, "L0_tok_bp"), (B_OUT, "L0_attn_b_out"), (B_FFN, "L0_ffn_bp")):
        biases[:, col:col + NCH] = twice(f[name]).reshape(NCH, 128).T
    for n in range(4):
        biases[:, B_QK + n] = np.concatenate([bqk[order[2 * n]], bqk[order[2 * n + 1]]])
    biases[0:HD, B_CONVW:B_CONVW + 3] = f["L0_ffn_conv_w"].reshape(HD, 3)
    biases[0:HD, B_CONVB] = f["L0_ffn_conv_b"]
    biases[0:32, B_G1] = f["L0_ffn_bg1"]
    pos_bias = np.zeros((128, TOK), np.float32)
    pos_bias[0:TOK] = pos_bias[64:64 + TOK] = f["L0_ffn_pos_bias"][0:TOK, 0:TOK]

    tok = np.arange(TOK)
    dist = tok[None, :] - tok[:, None]
    band, causal, outside = np.zeros((128, TOK)), np.zeros((128, TOK)), np.ones(128)
    for lo in (0, 64):
        band[lo:lo + TOK] = np.where(abs(dist) <= WINDOW_SIDE, 0.0, NEG)
        causal[lo:lo + TOK] = np.where(dist > 0, NEG, 0.0)
        outside[lo:lo + TOK] = 2 * WINDOW_SIDE + 1 - (abs(dist) <= WINDOW_SIDE).sum(1)
    consts = np.zeros((128, C_END), np.float32)
    consts[:, C_IDENT:C_IDENT + 128] = np.eye(128)
    consts[:, C_CAUSAL:C_CAUSAL + TOK] = causal
    consts[:, C_OUTSIDE] = outside
    consts[:, C_EPS] = 1e-5
    consts[:, C_MEAN:C_MEAN + 128] = 1.0 / DIM
    bf_consts = np.concatenate([np.eye(128), band, causal], axis=1).astype(ml_dtypes.bfloat16)

    arrays = {
        "x_t": x,
        "tok_w": twice(f["L0_tok_Wp"].T).reshape(PK, 128, DUP).transpose(1, 0, 2),
        "w_qk": w_qk,
        "w_v": chunks(qkv[:, :, :, 2].reshape(DIM, PATCH)),
        "w_out": twice(f["L0_attn_w_out"]).reshape(PAIRS, 128, DUP).transpose(1, 0, 2),
        "f_w": chunks(f_w),
        "f_g2": np.concatenate([f["L0_ffn_Wg2"], f["L0_ffn_bg2"][None]]),
        "f_bv": np.stack([f["L0_ffn_bv"].reshape(DIM)] * 128),
        "pos_bias": pos_bias, "biases": biases, "consts": consts, "bf_consts": bf_consts,
    }
    arrays = {k: np.ascontiguousarray(a) for k, a in arrays.items()}
    nc = bacc.Bacc("TRN2", target_bir_lowering=False, num_devices=1)
    args = [nc.dram_tensor(k, a.shape, mybir.dt.from_np(a.dtype), kind="ExternalInput").ap() for k, a in arrays.items()]
    out = nc.dram_tensor("out_t", (DIM, IMAGES * TOK), F32, kind="ExternalOutput").ap()
    vit_tower(nc, *args, out)
    got = run_bass_kernel_spmd(nc, [arrays], core_ids=[0]).results[0]["out_t"]
    return np.ascontiguousarray(got.T.reshape(IMAGES, TOK, DIM))
```

```python
from contextlib import ExitStack

import concourse.bass as bass
from concourse import mybir

F32 = mybir.dt.float32
F32R = mybir.dt.float32r
BF16 = mybir.dt.bfloat16
ALU = mybir.AluOpType
ACT = mybir.ActivationFunctionType
AX = mybir.AxisListType

IMAGES, TOK, SLOT = 16, 36, 64
GROUPS, GI = 2, 8
GT = GI * TOK
TILES = GI // 2
DIM, NCH = 192, 2
DUP = 256
PATCH, PK = 768, 6
PAIRS, HD = 6, 64
SCALE = 0.125
WINDOW_SIDE = 32
NEG = -1.0e30

C_IDENT, C_CAUSAL, C_OUTSIDE, C_EPS, C_MEAN = 0, 128, 164, 165, 166
C_END = C_MEAN + 128
B_TOK, B_OUT, B_FFN, B_QK, B_CONVW, B_CONVB, B_G1 = 0, 2, 4, 6, 10, 13, 14
B_END = 15

F_GATE = 512
F_VAL = F_GATE + 128
F_PROJ = F_VAL + DIM
F_END = F_PROJ + DUP
TOK_PIECES = [slice(0, 1), slice(1, 3), slice(3, 6)]
X_PIECES = [(0, ks) for ks in TOK_PIECES] + [(1, slice(0, 3)), (1, slice(3, 6))]

QK_STEPS = (0, 2, 3)
WARM_UP, WARM = 20, 8
QK_RING = 3

ENTRIES = ([("attn", g, p) for g in range(GROUPS) for p in range(PAIRS)]
           + [("ffn", g, p) for g in range(GROUPS) for p in range(2)])
ENTRY_OF = {e: n for n, e in enumerate(ENTRIES)}

ORDER = """
h 0, wts 0, qk 0, h 1, wts 1, qk 1, v 0 0, wts 2
v 0 1, s 0, norm 0, v 0 2, v 0 3, wts 3, qk 2, s 1
norm 1, t 0, wts 4, qk 3, s 2, t 1, pv 0, wts 5
norm 2, qk 4, pv 1, s 3, t 2, norm 3, v 1 0, pv 2
v 1 1, qk 5, s 4, t 3, v 1 2, v 1 3, norm 4, qk 6
pv 3, s 5, t 4, norm 5, qk 7, s 6, qk 8, t 5
norm 6, pv 4, pv 5, s 7, t 6, norm 7, out 0 0, out 0 1
s 8, pv 6, t 7, qk 9, norm 8, mean 0, qk 10, s 9
pv 7, t 8, norm 9, warm 0, var 0, pv 8, h1 0, qk 11
t 9, s 10, norm 10, gate 0, fv 0 0, fv 0 1, lg 0, qk 12
s 11, t 10, qk 13, norm 11, pv 9, pv 10, t 11, s 12
norm 12, pv 11, s 13, t 12, out 1 0, norm 13, out 1 1, pv 12
t 13, mean 1, pv 13, var 1, out2 0 0, out2 0 1, h1 1, mean2 0
qk 14, gate 1, fv 1 0, fv 1 1, lg 1, qk 15, warm 1, s 14
s 15, norm 14, var2 0, warm 2, h2 0, t 14, norm 15, pv 14
t 15, pv 15, out2 1 0, out2 1 1, mean2 1, var2 1, h2 1
"""
STEPS = [(w[0], *map(int, w[1:])) for w in (t.split() for t in ORDER.replace("\n", ",").split(",")) if w]


def vit_tower(nc, x_t, tok_w, w_qk, w_v, w_out, f_w, f_g2, f_bv, pos_bias, biases, consts, bf_consts, out_t):
    with ExitStack() as ctx:
        def sb(name, shape, dt=F32):
            return ctx.enter_context(nc.sbuf_tensor(name, shape, dt))

        def sem(name):
            return ctx.enter_context(nc.semaphore(name))

        x_f = sb("x_f", [128, GROUPS, PK, GT])
        x_hi = sb("x_hi", [128, GROUPS, PK, GT], F32R)
        x_lo = sb("x_lo", [128, GROUPS, PK, GT], F32R)
        tw_f = sb("tw_f", [128, PK, DUP])
        tw_hi = sb("tw_hi", [128, PK, DUP], F32R)
        tw_lo = sb("tw_lo", [128, PK, DUP], F32R)
        wqk_f = sb("wqk_f", [128, PAIRS, NCH, 256])
        wqk_hi = sb("wqk_hi", [128, PAIRS, NCH, 256], F32R)
        wqk_lo = sb("wqk_lo", [128, PAIRS, 256], F32R)
        wv_f = sb("wv_f", [128, NCH, PATCH])
        wv_hi = sb("wv_hi", [128, NCH, PATCH], F32R)
        wv_lo = sb("wv_lo", [128, PATCH], F32R)
        wo_f = sb("wo_f", [128, PAIRS, DUP])
        wo_hi = sb("wo_hi", [128, PAIRS, DUP], F32R)
        wo_lo = sb("wo_lo", [128, PAIRS, DUP], F32R)
        ffn_f = sb("ffn_f", [128, NCH, F_END])
        ffn_hi = sb("ffn_hi", [128, NCH, F_END], F32R)
        ffn_lo = sb("ffn_lo", [128, F_END], F32R)
        fg2_w = sb("fg2_w", [33, 3])
        bv_all = sb("bv_all", [128, DIM])
        bias = sb("bias", [128, B_END])
        const = sb("const", [128, C_END])
        bfc = sb("bfc", [128, 128 + 2 * TOK], BF16)
        zeros = sb("zeros", [128, 256], BF16)
        posb = sb("posb", [128, TOK])
        posmask = sb("posmask", [128, TOK])
        ident = const[:, C_IDENT:C_IDENT + 128]
        outside = const[:, C_OUTSIDE:C_OUTSIDE + 1]
        eps = const[:, C_EPS:C_EPS + 1]
        mean_w = const[:, C_MEAN:C_MEAN + 128]
        ident_bf = bfc[:, 0:128]
        band_bf = bfc[:, 128:128 + TOK]
        causal_bf = bfc[:, 128 + TOK:128 + 2 * TOK]

        h_f = sb("h_f", [128, NCH, GROUPS, GT])
        h_hi = sb("h_hi", [128, NCH, IMAGES, SLOT], F32R)
        h_lo = sb("h_lo", [128, NCH, IMAGES, SLOT], F32R)
        n_seq = len(ENTRIES)
        q_t = sb("q_t", [128, QK_RING, GT])
        k_t = sb("k_t", [128, QK_RING, GT])
        qc_t = sb("qc_t", [HD, 2, GT])
        v_t = [sb("v_t", [128, TILES, PATCH])[:],
               x_f[:].rearrange("p g k t -> p (g k t)")[:, 0:TILES * PATCH].rearrange("p (j d) -> p j d", d=PATCH)]
        fv_t = wv_f[:].rearrange("p c (j d) -> p (c j) d", d=DIM)
        d_t = sb("d_t", [128, 2, GI, TOK])
        e_t = sb("e_t", [128, 2, GI, TOK])
        p_t = sb("p_t", [128, 2, GI, SLOT])
        pt_t = sb("pt_t", [128, 2, TILES, 2, 2, TOK])
        mx_t = sb("mx_t", [128, n_seq, 2, GI])
        z_t = sb("z_t", [128, n_seq, GI])
        sm_t = sb("sm_t", [128, n_seq, 3, GI])
        o_hi = x_hi
        o_lo = x_lo
        y_hi, y_lo = (t[:].rearrange("p k d -> p (k d)")[:, 0:GROUPS * 2 * GT].rearrange(
            "p (g c t) -> p g c t", g=GROUPS, c=2) for t in (tw_hi, tw_lo))
        r_t, c_t, sq_t, ln_t = (
            wqk_f[:].rearrange("p a c d -> p (a c d)")[:, n * NCH * GT:(n + 1) * NCH * GT].rearrange(
                "p (c t) -> p c t", c=NCH) for n in range(4))
        g1_t = sb("g1_t", [33, GI, 2, SLOT])
        n_ln, n_gm = 4 * NCH * GT, GROUPS * 8 * GI * 3
        gate_room = wqk_f[:].rearrange("p a c d -> p (a c d)")[:, n_ln:n_ln + n_gm + GROUPS * 8 * GI]
        gm = gate_room[:, 0:n_gm].rearrange("p (g z i e) -> p g z i e", g=GROUPS, z=8, e=3)
        gs = gate_room[:, n_gm:].rearrange("p (g z i) -> p g z i", g=GROUPS, z=8)
        wgt = sb("wgt", [128, GROUPS, 2, GI])
        out_s = tw_f[:].rearrange("p k d -> p (k d)")[:, 0:GROUPS * NCH * GT].rearrange(
            "p (g c t) -> p g c t", g=GROUPS, c=NCH)

        proj = [ctx.enter_context(nc.psum_tensor(f"proj{i}", [128, 512], F32)) for i in range(3)]
        score = [ctx.enter_context(nc.psum_tensor(f"score{i}", [128, 512], F32)) for i in range(2)]
        trans = ctx.enter_context(nc.psum_tensor("trans", [128, TILES, 2, SLOT], F32))
        outp = [ctx.enter_context(nc.psum_tensor(f"outp{i}", [128, 512], F32)) for i in range(2)]
        embed_bank = [[proj[0], proj[1]], [score[0], score[1]]]

        ld_const, ld_wv, ld_wo, ld_ffn, ld_small = (sem(s) for s in ("ld_const", "ld_wv", "ld_wo", "ld_ffn", "ld_small"))
        ld_x = [sem(f"ld_x{n}") for n in range(len(X_PIECES))]
        ld_tok = [sem(f"ld_tok{n}") for n in range(len(TOK_PIECES))]
        ld_qk = [sem(f"ld_qk{p}") for p in range(PAIRS // 2)]
        ld_bias = sem("ld_bias")
        st_out, zeros_s = sem("st_out"), sem("zeros_s")
        zeroed = sem("zeroed")
        tok_hi, tok_lo, x_hi_s, x_lo_s = (sem(s) for s in ("tok_hi", "tok_lo", "x_hi_s", "x_lo_s"))
        qk_hi, qk_lo, wv_hi_s, wv_lo_s, wo_hi_s, wo_lo_s = (
            sem(s) for s in ("qk_hi", "qk_lo", "wv_hi_s", "wv_lo_s", "wo_hi_s", "wo_lo_s"))
        posmask_s = sem("posmask_s")
        ffn_hi_s, ffn_lo_s, h1_hi_s, h1_lo_s = (sem(s) for s in ("ffn_hi_s", "ffn_lo_s", "h1_hi_s", "h1_lo_s"))
        embedded = sem("embedded")
        h_hi_s, h_f_s, h_lo_s = (sem(s) for s in ("h_hi_s", "h_f_s", "h_lo_s"))
        projected = sem("projected")
        scored = sem("scored")
        transposed = sem("transposed")
        attended = sem("attended")
        q_s, k_s = sem("q_s"), sem("k_s")
        v_s = sem("v_s")
        shifted, exped, zeroed_key, normed, pt_a, pt_d = (
            sem(s) for s in ("shifted", "exped", "outside_exped", "normed", "pt_a", "pt_d"))
        o_hi_s, o_lo_s = sem("o_hi_s"), sem("o_lo_s")
        res_s, cen_s, sq_s, rstd_s, h1_s = (sem(s) for s in ("res_s", "cen_s", "sq_s", "rstd_s", "h1_s"))
        g1_s, gate_exp, gate_exp2, gated, conv_s, fv_s = (
            sem(s) for s in ("g1_s", "gate_exp", "gate_exp2", "gated", "conv_s", "fv_s"))
        gate_d, gate_g, logit_s = sem("gate_d"), sem("gate_g"), sem("logit_s")
        outs, scaled = sem("outs"), sem("scaled")
        dve_chain, act_chain = sem("dve_chain"), sem("act_chain")

        uses, freed_by = {}, []

        def plan(kind, key, freed):
            uses[(kind, key)] = len(freed_by)
            freed_by.append(freed)

        norms = [(w[0], w[1]) for w in STEPS if w[0] in ("mean", "mean2")]
        n_of = {}
        for kind, g in norms:
            layer = kind[4:]
            for part in ("out", "mean", "var"):
                n_of[(part + layer, g)] = norms.index((kind, g))
            n_of[("h" + (layer or "1"), g)] = norms.index((kind, g))
        n_res = n_v = n_fv = 0
        for w in STEPS:
            kind, key = w[0], w[1:] if len(w) > 2 else w[1]
            if kind == "qk":
                plan("q", key, (q_s, key + 1))
                plan("k", key, (k_s, key + 1))
            elif kind == "v":
                for half in range(2):
                    n_v += 1
                    plan("v", (*key, half), (v_s, n_v))
            elif kind in ("out", "out2"):
                n_res += 1
                plan(kind, key, (res_s, n_res))
            elif kind in ("mean", "mean2"):
                plan(kind, key, (cen_s, n_of[(kind, key)] + 1))
            elif kind in ("var", "var2"):
                plan(kind, key, (rstd_s, n_of[(kind, key)] + 1))
            elif kind == "gate":
                plan("g1", key, (g1_s, 2 * key + 2))
            elif kind == "fv":
                n_fv += 1
                plan("fv", key, (fv_s, n_fv))
            elif kind == "lg":
                plan("lg", key, (logit_s, key + 1))
            elif kind == "warm":
                plan("warm", key, (projected, len(freed_by) + 1))

        def bank(kind, key):
            return proj[uses[(kind, key)] % 3]

        def hcols(t, g, c, rows=128):
            return t[0:rows, c, GI * g:GI * g + GI, 0:TOK]

        def by_image(ap):
            return ap.rearrange("p (i t) -> p i t", t=TOK)

        ZEROED = 6
        block = ctx.enter_context(nc.Block())

        @block.sync
        def _(sp):
            for n, ks in enumerate(TOK_PIECES):
                sp.dma_start(tw_f[:, ks], tok_w[:, ks]).then_inc(ld_tok[n], 16)
                sp.dma_start(x_f[:, 0, ks], x_t[:, 0, ks]).then_inc(ld_x[n], 16)
            for n, (g, ks) in enumerate(X_PIECES):
                if g:
                    sp.dma_start(x_f[:, g, ks], x_t[:, g, ks]).then_inc(ld_x[n], 16)
            sp.dma_start(bias[:], biases).then_inc(ld_bias, 16)
            for n in range(PAIRS // 2):
                sp.dma_start(wqk_f[:, 2 * n:2 * n + 2], w_qk[:, 2 * n:2 * n + 2]).then_inc(ld_qk[n], 16)
                if n == 0:
                    sp.dma_start(wv_f[:], w_v).then_inc(ld_wv, 16)
                    sp.dma_start(bfc[:], bf_consts).then_inc(ld_const, 16)
                    sp.dma_start(const[:], consts).then_inc(ld_const, 16)
            sp.dma_start(wo_f[:], w_out).then_inc(ld_wo, 16)
            sp.dma_start(ffn_f[:], f_w).then_inc(ld_ffn, 16)
            sp.dma_start(fg2_w[:], f_g2).then_inc(ld_small, 16)
            sp.dma_start(bv_all[:], f_bv).then_inc(ld_small, 16)
            sp.dma_start(posb[:], pos_bias).then_inc(ld_small, 16)
            for n, g in enumerate((0, 1)):
                cols = slice(g * GT, (g + 1) * GT)
                sp.wait_ge(outs, NCH * n + 1)
                sp.dma_start(out_t[0:128, cols], out_s[:, g, 0]).then_inc(st_out, 16)
                sp.wait_ge(outs, NCH * n + 2)
                sp.dma_start(out_t[128:DIM, cols], out_s[0:64, g, 1]).then_inc(st_out, 16)
            sp.wait_ge(st_out, 32 * GROUPS)

        @block.gpsimd
        def _(pool):
            for t in (h_hi, h_lo, p_t, pt_t, g1_t):
                pool.memset(t[:].bitcast(F32), 0.0).then_inc(zeroed, 1)
            pool.wait_ge(zeroed, 5)
            pool.memset(g1_t[32:33], 1.0).then_inc(zeroed, 1)
            pool.wait_ge(zeroed, 6)

            def lo_part(lo, hi, raw, done, before):
                nc.gpsimd.tensor_tensor(lo, raw[:, 0], hi[:, 0].bitcast(F32), ALU.subtract).then_inc(done, 1)
                pool.wait_ge(done, before + 1)
                nc.gpsimd.tensor_tensor(hi[64:128, 1], raw[64:128, 1], hi[64:128, 1].bitcast(F32),
                                        ALU.subtract).then_inc(done, 1)
                pool.wait_ge(done, before + 2)

            for p in range(PAIRS):
                pool.wait_ge(qk_hi, p // 2 + 1)
                lo_part(wqk_lo[:, p], wqk_hi[:, p], wqk_f[:, p], qk_lo, 2 * p)
            pool.wait_ge(wo_hi_s, 1)
            nc.gpsimd.tensor_tensor(wo_lo[:], wo_f[:], wo_hi[:].bitcast(F32), ALU.subtract).then_inc(wo_lo_s, 1)
            pool.wait_ge(wo_lo_s, 1)
            pool.wait_ge(ffn_hi_s, 1)
            lo_part(ffn_lo[:], ffn_hi[:], ffn_f[:], ffn_lo_s, 0)

        @block.scalar
        def _(act):
            act.preload_act_table_set("natural_log_exp_and_others")
            for n, (g, ks) in enumerate(X_PIECES):
                if g == 0:
                    act.wait_ge(ld_tok[n], 16)
                    nc.scalar.activation(tw_hi[:, ks], tw_f[:, ks], ACT.Copy).then_inc(tok_hi, 1)
                act.wait_ge(ld_x[n], 16)
                nc.scalar.activation(x_hi[:, g, ks], x_f[:, g, ks], ACT.Copy).then_inc(x_hi_s, 1)

            def raw_hi(n):
                act.wait_ge(ld_qk[n], 16)
                nc.scalar.activation(wqk_hi[:, 2 * n:2 * n + 2], wqk_f[:, 2 * n:2 * n + 2],
                                     ACT.Copy).then_inc(qk_hi, 1)

            def embedding_hi(g):
                act.wait_ge(ld_bias, 16)
                act.wait_ge(zeroed, ZEROED)
                for m in range(NCH):
                    act.wait_ge(embedded, NCH * g + m + 1)
                    nc.scalar.activation(hcols(h_hi, g, m), by_image(embed_bank[g][m][:, 0:GT]), ACT.Identity,
                                         bias=bias[:, B_TOK + m:B_TOK + m + 1]).then_inc(h_hi_s, 1)

            def copy_q_k(n):
                kind, g, p = ENTRIES[n]
                if n >= QK_RING:
                    act.wait_ge(scored, n - QK_RING + 1)
                for which, (dst, name, done) in enumerate(((q_t, "q", q_s), (k_t, "k", k_s))):
                    act.wait_ge(projected, uses[(name, n)] + 1)
                    b = bank(name, n)[:, 0:GT]
                    if kind == "attn":
                        nc.scalar.activation(dst[:, n % QK_RING], b, ACT.Copy).then_inc(done, 1)
                    else:
                        col = B_QK + 2 * p + which
                        nc.scalar.activation(dst[:, n % QK_RING], b, ACT.Identity, bias=bias[:, col:col + 1]).then_inc(done, 1)

            def exp_scores(n):
                if n >= 2:
                    act.wait_ge(normed, n - 1)
                act.wait_ge(shifted, n + 1)
                nc.scalar.activation(e_t[:, n % 2], d_t[:, n % 2], ACT.Exp, scale=SCALE).then_inc(exped, 1)
                if ENTRIES[n][0] == "attn":
                    nc.scalar.activation(z_t[:, n], mx_t[:, n, 1], ACT.Exp, scale=-SCALE).then_inc(zeroed_key, 1)

            def copy_transposed(n):
                act.wait_ge(transposed, n + 1)
                if n >= 2:
                    act.wait_ge(attended, n - 1)
                nc.scalar.activation(pt_t[0:64, n % 2, :, :, 0], trans[0:64, :, :, 0:TOK], ACT.Copy).then_inc(pt_a, 1)

            def copy_outputs(n):
                kind, g, p = ENTRIES[n]
                act.wait_ge(attended, n + 1)
                dst = o_hi[:, g, p] if kind == "attn" else y_hi[:, g, p]
                nc.scalar.activation(dst, outp[n % 2][:, 0:GT], ACT.Copy).then_inc(o_hi_s, 1)

            def weights_hi(n):
                if n in QK_STEPS:
                    raw_hi(QK_STEPS.index(n))
                elif n == 1:
                    act.wait_ge(ld_wv, 16)
                    nc.scalar.activation(wv_hi[:], wv_f[:], ACT.Copy).then_inc(wv_hi_s, 1)
                elif n == 4:
                    act.wait_ge(ld_wo, 16)
                    nc.scalar.activation(wo_hi[:], wo_f[:], ACT.Copy).then_inc(wo_hi_s, 1)
                else:
                    act.wait_ge(ld_ffn, 16)
                    nc.scalar.activation(ffn_hi[:], ffn_f[:], ACT.Copy).then_inc(ffn_hi_s, 1)

            def copy_values(g, j):
                for half in range(2):
                    u = (g, j, half)
                    act.wait_ge(projected, uses[("v", u)] + 1)
                    nc.scalar.activation(v_t[g][:, j, 384 * half:384 * half + 384], bank("v", u)[:, 0:384],
                                         ACT.Copy).then_inc(v_s, 1)

            def square(kind, g):
                act.wait_ge(cen_s, n_of[(kind, g)] + 1)
                nc.scalar.activation(sq_t, c_t, ACT.Square).then_inc(sq_s, 1)

            def inverse_deviation(kind, g):
                n = n_of[(kind, g)]
                act.wait_ge(projected, uses[(kind, g)] + 1)
                nc.scalar.activation(ln_t[:, 0], bank(kind, g)[:, 0:GT], ACT.Ln, bias=eps).then_inc(act_chain, 1)
                act.wait_ge(act_chain, n + 1)
                nc.scalar.activation(ln_t[:, 1], ln_t[:, 0], ACT.Exp, scale=-0.5).then_inc(rstd_s, 1)

            def split_h1(g):
                for m in range(NCH):
                    act.wait_ge(h1_s, NCH * g + m + 1)
                    nc.scalar.activation(hcols(h_hi, g, m), by_image(h_f[:, m, g]), ACT.Copy).then_inc(h1_hi_s, 1)

            def gate_hidden(g):
                act.wait_ge(projected, uses[("g1", g)] + 1)
                src = by_image(bank("g1", g)[0:32, 0:GT])
                if g:
                    act.wait_ge(logit_s, g)
                for dup in range(2):
                    nc.scalar.activation(g1_t[0:32, :, dup, 0:TOK], src, ACT.Relu,
                                         bias=bias[0:32, B_G1:B_G1 + 1]).then_inc(g1_s, 1)

            def gate_exps(g):
                act.wait_ge(gate_d, g + 1)
                nc.scalar.activation(gm[:, g, 1], gm[:, g, 0], ACT.Exp).then_inc(gate_exp, 1)
                act.wait_ge(gate_g, g + 1)
                nc.scalar.activation(gm[:, g, 4], gm[:, g, 3], ACT.Exp).then_inc(gate_exp2, 1)

            for kind, *a in STEPS:
                if kind == "qk":
                    copy_q_k(*a)
                elif kind == "s":
                    exp_scores(*a)
                elif kind == "t":
                    copy_transposed(*a)
                elif kind == "pv":
                    copy_outputs(*a)
                elif kind == "v":
                    copy_values(*a)
                elif kind == "wts":
                    weights_hi(*a)
                elif kind == "h":
                    embedding_hi(*a)
                elif kind in ("mean", "mean2"):
                    square(kind, *a)
                elif kind in ("var", "var2"):
                    inverse_deviation(kind, *a)
                elif kind == "h1":
                    split_h1(*a)
                elif kind == "gate":
                    gate_hidden(*a)
                elif kind == "lg":
                    gate_exps(*a)

        @block.vector
        def _(dve):
            nc.vector.memset(zeros[:], 0.0).then_inc(zeros_s, 1)
            chain = [0]

            def link(ins):
                chain[0] += 1
                ins.then_inc(dve_chain, 1)
                dve.wait_ge(dve_chain, chain[0])

            for n, (g, ks) in enumerate(X_PIECES):
                if g == 0:
                    dve.wait_ge(tok_hi, n + 1)
                    nc.vector.tensor_tensor(tw_lo[:, ks], tw_f[:, ks], tw_hi[:, ks].bitcast(F32),
                                            ALU.subtract).then_inc(tok_lo, 1)
                dve.wait_ge(x_hi_s, n + 1)
                nc.vector.tensor_tensor(x_lo[:, g, ks], x_f[:, g, ks], x_hi[:, g, ks].bitcast(F32),
                                        ALU.subtract).then_inc(x_lo_s, 1)

            def values_lo():
                dve.wait_ge(wv_hi_s, 1)
                nc.vector.tensor_tensor(wv_lo[:], wv_f[:, 0], wv_hi[:, 0].bitcast(F32),
                                        ALU.subtract).then_inc(wv_lo_s, 1)
                nc.vector.tensor_tensor(wv_hi[64:128, 1], wv_f[64:128, 1], wv_hi[64:128, 1].bitcast(F32),
                                        ALU.subtract).then_inc(wv_lo_s, 1)

            def embedding_lo(g):
                for m in range(NCH):
                    n = NCH * g + m
                    dve.wait_ge(h_hi_s, n + 1)
                    nc.vector.tensor_scalar(h_f[:, m, g], embed_bank[g][m][:, 0:GT],
                                            bias[:, B_TOK + m:B_TOK + m + 1], None, ALU.add).then_inc(h_f_s, 1)
                    dve.wait_ge(h_f_s, n + 1)
                    nc.vector.tensor_tensor(hcols(h_lo, g, m), by_image(h_f[:, m, g]),
                                            hcols(h_hi, g, m).bitcast(F32), ALU.subtract).then_inc(h_lo_s, 1)

            def position_mask():
                dve.wait_ge(ld_small, 16 * 3)
                dve.wait_ge(ld_const, 32)
                nc.vector.scalar_tensor_tensor(out=posmask[:], in0=posb[:], scalar=1.0 / SCALE,
                                               in1=const[:, C_CAUSAL:C_CAUSAL + TOK], op0=ALU.mult,
                                               op1=ALU.add).then_inc(posmask_s, 1)

            def shift_scores(n):
                kind, g, p = ENTRIES[n]
                s = by_image(score[n % 2][:, 0:GT])
                dve.wait_ge(scored, n + 1)
                if kind == "attn":
                    link(nc.vector.tensor_reduce(mx_t[:, n, 0], s, AX.X, ALU.max))
                    link(nc.vector.tensor_scalar(mx_t[:, n, 1], mx_t[:, n, 0], 0.0, None, ALU.max))
                else:
                    link(nc.vector.tensor_reduce(mx_t[:, n, 1], s, AX.X, ALU.max))
                if n >= 2:
                    dve.wait_ge(exped, n - 1)
                nc.vector.tensor_tensor(d_t[:, n % 2], s, mx_t[:, n, 1].unsqueeze(2).broadcast_to([128, GI, TOK]),
                                        ALU.subtract).then_inc(shifted, 1)

            def normalise(n):
                kind, g, p = ENTRIES[n]
                dve.wait_ge(exped, n + 1)
                link(nc.vector.tensor_reduce(sm_t[:, n, 0], e_t[:, n % 2], AX.X, ALU.add))
                if kind == "attn":
                    dve.wait_ge(zeroed_key, n + 1 if n < 12 else 12)
                    link(nc.vector.scalar_tensor_tensor(out=sm_t[:, n, 1], in0=z_t[:, n], scalar=outside,
                                                        in1=sm_t[:, n, 0], op0=ALU.mult, op1=ALU.add))
                    link(nc.vector.reciprocal(sm_t[:, n, 2], sm_t[:, n, 1]))
                else:
                    link(nc.vector.reciprocal(sm_t[:, n, 1], sm_t[:, n, 0]))
                    dve.wait_ge(gated, 3 * g + 3)
                    link(nc.vector.tensor_tensor(sm_t[:, n, 2], sm_t[:, n, 1], wgt[:, g, p], ALU.mult))
                if n >= 2:
                    dve.wait_ge(transposed, n - 1)
                nc.vector.tensor_tensor(p_t[:, n % 2, :, 0:TOK], e_t[:, n % 2],
                                        sm_t[:, n, 2].unsqueeze(2).broadcast_to([128, GI, TOK]),
                                        ALU.mult).then_inc(normed, 1)

            def copy_transposed(n):
                dve.wait_ge(transposed, n + 1)
                if n >= 2:
                    dve.wait_ge(attended, n - 1)
                nc.vector.tensor_copy(pt_t[64:128, n % 2, :, :, 1], trans[64:128, :, :, 0:TOK]).then_inc(pt_d, 1)

            def outputs_lo(n):
                kind, g, p = ENTRIES[n]
                dve.wait_ge(o_hi_s, n + 1)
                hi, lo = (o_hi[:, g, p], o_lo[:, g, p]) if kind == "attn" else (y_hi[:, g, p], y_lo[:, g, p])
                nc.vector.tensor_tensor(lo, outp[n % 2][:, 0:GT], hi.bitcast(F32), ALU.subtract).then_inc(o_lo_s, 1)

            def convolve(n):
                g = ENTRIES[n][1]
                dve.wait_ge(q_s, n + 1)
                if g:
                    dve.wait_ge(scored, n)
                q = by_image(q_t[0:HD, n % QK_RING])
                a, b = (by_image(qc_t[:, z]) for z in range(2))
                w = [bias[0:HD, B_CONVW + j:B_CONVW + j + 1] for j in range(3)]
                link(nc.vector.tensor_scalar(a, q, w[1], bias[0:HD, B_CONVB:B_CONVB + 1], ALU.mult, ALU.add))
                nc.vector.tensor_copy(b[:, :, 0:1], a[:, :, 0:1])
                link(nc.vector.scalar_tensor_tensor(out=b[:, :, 1:TOK], in0=q[:, :, 0:TOK - 1], scalar=w[0],
                                                    in1=a[:, :, 1:TOK], op0=ALU.mult, op1=ALU.add))
                link(nc.vector.tensor_copy(a[:, :, TOK - 1:TOK], b[:, :, TOK - 1:TOK]))
                nc.vector.scalar_tensor_tensor(out=a[:, :, 0:TOK - 1], in0=q[:, :, 1:TOK], scalar=w[2],
                                               in1=b[:, :, 0:TOK - 1], op0=ALU.mult, op1=ALU.add).then_inc(conv_s, 1)

            def gate(g):
                t = [gm[:, g, z] for z in range(8)]
                s = [gs[:, g, z] for z in range(8)]
                wide = lambda z: z.unsqueeze(2).broadcast_to([128, GI, 3])
                dve.wait_ge(projected, uses[("lg", g)] + 1)
                lg = bank("lg", g)[:, 0:3 * GI].rearrange("p (i e) -> p i e", e=3)
                link(nc.vector.tensor_reduce(s[0], lg, AX.X, ALU.max))
                link(nc.vector.tensor_tensor(t[0], lg, wide(s[0]), ALU.subtract))
                dve.sem_inc(gate_d, 1)
                dve.sem_inc(logit_s, 1)
                dve.wait_ge(gate_exp, g + 1)
                link(nc.vector.tensor_reduce(s[1], t[1], AX.X, ALU.add))
                link(nc.vector.reciprocal(s[2], s[1]))
                link(nc.vector.tensor_tensor(t[2], t[1], wide(s[2]), ALU.mult))
                link(nc.vector.tensor_reduce(s[3], t[2], AX.X, ALU.max))
                nc.vector.tensor_tensor(t[3], t[2], wide(s[3]), ALU.subtract).then_inc(gate_g, 1)
                g0, g1, g2 = (t[2][:, :, z] for z in range(3))
                nc.vector.tensor_tensor(s[4], g0, g1, ALU.min)
                link(nc.vector.tensor_tensor(s[5], g1, g2, ALU.min))
                keep = t[5]
                nc.vector.tensor_tensor(keep[:, :, 2], g2, s[4], ALU.is_gt)
                link(nc.vector.tensor_tensor(keep[:, :, 0], g0, s[5], ALU.is_ge))
                link(nc.vector.tensor_tensor(s[6], keep[:, :, 0], keep[:, :, 2], ALU.add))
                link(nc.vector.tensor_scalar(keep[:, :, 1], s[6], -1.0, 2.0, ALU.mult, ALU.add))
                dve.wait_ge(gate_exp2, g + 1)
                link(nc.vector.tensor_tensor(t[6], t[4], keep, ALU.mult))
                link(nc.vector.tensor_reduce(s[7], t[6], AX.X, ALU.add))
                link(nc.vector.reciprocal(s[0], s[7]))
                link(nc.vector.tensor_tensor(t[7], t[6], wide(s[0]), ALU.mult))
                nc.vector.tensor_copy(wgt[0:64, g, 0], t[7][0:64, :, 0]).then_inc(gated, 1)
                nc.vector.tensor_copy(wgt[64:128, g, 0], t[7][64:128, :, 1]).then_inc(gated, 1)
                nc.vector.tensor_copy(wgt[:, g, 1], t[7][:, :, 2]).then_inc(gated, 1)

            def residual(kind, g, m):
                n = n_of[(kind, g)]
                if n:
                    dve.wait_ge(cen_s, n)
                dve.wait_ge(projected, uses[(kind, (g, m))] + 1)
                col = (B_OUT if kind == "out" else B_FFN) + m
                nc.vector.scalar_tensor_tensor(out=r_t[:, m], in0=bank(kind, (g, m))[:, 0:GT],
                                               scalar=bias[:, col:col + 1], in1=h_f[:, m, g], op0=ALU.add,
                                               op1=ALU.add).then_inc(res_s, 1)

            def centre(kind, g):
                n = n_of[(kind, g)]
                dve.wait_ge(projected, uses[(kind, g)] + 1)
                if n:
                    dve.wait_ge(sq_s, n)
                    dve.wait_ge(scaled, NCH * n)
                nc.vector.tensor_tensor(c_t, r_t, bank(kind, g)[:, 0:GT].unsqueeze(1).broadcast_to([128, NCH, GT]),
                                        ALU.subtract).then_inc(cen_s, 1)

            def scale(kind, g):
                n = n_of[(kind, g)]
                dve.wait_ge(rstd_s, n + 1)
                for m in range(NCH):
                    dst = h_f[:, m, g] if kind == "h1" else out_s[:, g, m]
                    nc.vector.tensor_tensor(dst, c_t[:, m], ln_t[:, 1], ALU.mult).then_inc(
                        h1_s if kind == "h1" else outs, 1)
                    dve.sem_inc(scaled, 1)
                if kind == "h1":
                    for m in range(NCH):
                        dve.wait_ge(h1_hi_s, NCH * g + m + 1)
                        nc.vector.tensor_tensor(hcols(h_lo, g, m), by_image(h_f[:, m, g]),
                                                hcols(h_hi, g, m).bitcast(F32), ALU.subtract).then_inc(h1_lo_s, 1)

            def expert_values(g, z):
                dve.wait_ge(projected, uses[("fv", (g, z))] + 1)
                src = bank("fv", (g, z))[:, 0:2 * DIM].rearrange("p (j d) -> p j d", d=DIM)
                nc.vector.tensor_tensor(fv_t[:, TILES * g + 2 * z:TILES * g + 2 * z + 2], src,
                                        bv_all[:].unsqueeze(1).broadcast_to([128, 2, DIM]), ALU.add).then_inc(fv_s, 1)

            for kind, *a in STEPS:
                if kind == "qk" and ENTRIES[a[0]][0::2] == ("ffn", 0):
                    convolve(*a)
                elif kind == "s":
                    shift_scores(*a)
                elif kind == "norm":
                    normalise(*a)
                elif kind == "t":
                    copy_transposed(*a)
                elif kind == "pv":
                    outputs_lo(*a)
                elif kind in ("out", "out2"):
                    residual(kind, *a)
                elif kind in ("mean", "mean2"):
                    centre(kind, *a)
                elif kind in ("h1", "h2"):
                    scale(kind, *a)
                elif kind == "fv":
                    expert_values(*a)
                elif kind == "lg":
                    gate(*a)
                elif kind == "h":
                    dve.wait_ge(ld_bias, 16)
                    embedding_lo(*a)
                elif kind == "wts" and a[0] == 1:
                    values_lo()
                elif kind == "wts" and a[0] == 5:
                    position_mask()

        @block.tensor
        def _(pe):
            def features(out, w_hi, w_lo, h, tokens_first=False):
                ops = [(w_hi[:, 0], h(h_hi, 0, 128)), (w_hi[:, 0], h(h_lo, 0, 128)), (w_lo, h(h_hi, 0, 128)),
                       (w_hi[:, 1], h(h_hi, 1, 128)), (w_hi[0:64, 1], h(h_lo, 1, 64))]
                for n, (a, b) in enumerate(ops):
                    if tokens_first:
                        a, b = b, a
                    ins = nc.tensor.matmul(out, a, b, start=(n == 0), stop=(n == len(ops) - 1))
                return ins

            def take(kind, key):
                n = uses[(kind, key)]
                if n >= 3:
                    pe.wait_ge(*freed_by[n - 3])
                return proj[n % 3]

            def warm(n, count):
                b = take("warm", n)
                for _ in range(count):
                    ins = nc.tensor.matmul(b[:, 0:256], zeros[:, 0:128], zeros[:], start=True, stop=True)
                ins.then_inc(projected, 1)

            pe.wait_ge(zeros_s, 1)
            for _ in range(WARM_UP):
                nc.tensor.matmul(outp[0][:, 0:256], zeros[:, 0:128], zeros[:], start=True, stop=True)
            for n, (g, ks) in enumerate(X_PIECES):
                pe.wait_ge(x_lo_s, n + 1)
                if g == 0:
                    pe.wait_ge(tok_lo, n + 1)
                for k in range(ks.start, ks.stop):
                    for m in range(NCH):
                        cols = slice(128 * m, 128 * m + 128)
                        for z, (a, b) in enumerate(((tw_hi, x_hi), (tw_hi, x_lo), (tw_lo, x_hi))):
                            ins = nc.tensor.matmul(embed_bank[g][m][:, 0:GT], a[:, k, cols], b[:, g, k],
                                                   start=(k == 0 and z == 0), stop=(k == PK - 1 and z == 2))
                        if k == PK - 1:
                            ins.then_inc(embedded, 1)
            pe.wait_ge(zeroed, ZEROED)

            def project_qk(n):
                kind, g, p = ENTRIES[n]
                if kind == "attn":
                    pe.wait_ge(qk_lo, 2 * p + 2)
                    pe.wait_ge(h_lo_s, NCH * g + NCH)
                    pe.wait_ge(h_hi_s, NCH * g + NCH)
                    w_hi, w_lo = wqk_hi[:, p], wqk_lo[:, p]
                else:
                    pe.wait_ge(h1_lo_s, NCH * g + NCH)
                    pe.wait_ge(ffn_lo_s, 2)
                    w_hi, w_lo = (w[..., 256 * p:256 * p + 256] for w in (ffn_hi, ffn_lo))
                for which, name in enumerate("qk"):
                    b = take(name, n)
                    cols = slice(128 * which, 128 * which + 128)
                    features(by_image(b[:, 0:GT]), w_hi[:, :, cols], w_lo[:, cols],
                             lambda t, c, rows: hcols(t, g, c, rows)).then_inc(projected, 1)

            def scores(n):
                kind, g, p = ENTRIES[n]
                out = by_image(score[n % 2][:, 0:GT])
                pe.wait_ge(k_s, n + 1)
                pe.wait_ge(q_s, n + 1)
                if n == 0:
                    pe.wait_ge(h_lo_s, NCH * GROUPS)
                    pe.wait_ge(ld_const, 32)
                if n >= 2:
                    pe.wait_ge(shifted, n - 1)
                if (kind, p) == ("ffn", 0):
                    pe.wait_ge(conv_s, g + 1)
                if (kind, p) == ("ffn", 1):
                    pe.wait_ge(posmask_s, 1)
                    idn, mask = ident, posmask[:]
                else:
                    idn, mask = ident_bf, band_bf if kind == "attn" else causal_bf
                nc.tensor.matmul(out, idn, mask.unsqueeze(1).broadcast_to([128, GI, TOK]), start=True, stop=False,
                                 skip_group_check=True)
                for im in range(GI):
                    cols = slice(TOK * im, TOK * im + TOK)
                    for h in range(2):
                        rows = slice(HD * h, HD * h + HD)
                        q = qc_t[:, 0, cols] if (kind, p, h) == ("ffn", 0, 0) else q_t[rows, n % QK_RING, cols]
                        ins = nc.tensor.matmul(score[n % 2][64 * h:64 * h + TOK, cols], q, k_t[rows, n % QK_RING, cols],
                                               start=False, stop=True, skip_group_check=True)
                ins.then_inc(scored, 1)

            def transposes(n):
                pe.wait_ge(normed, n + 1)
                if n >= 1:
                    pe.wait_ge(pt_a, n)
                    pe.wait_ge(pt_d, n)
                for j in range(TILES):
                    src = p_t[:, n % 2, 2 * j:2 * j + 2, :].rearrange("p i s -> p (i s)")
                    ins = nc.tensor.transpose(trans[:, j].rearrange("p h s -> p (h s)"), src, ident)
                ins.then_inc(transposed, 1)

            def outputs(n):
                kind, g, p = ENTRIES[n]
                pe.wait_ge(pt_a, n + 1)
                pe.wait_ge(pt_d, n + 1)
                if n >= 2:
                    pe.wait_ge(o_lo_s, n - 1)
                if kind == "attn":
                    pe.wait_ge(v_s, 2 * TILES * (g + 1))
                else:
                    pe.wait_ge(fv_s, 2 * g + 2)
                val = v_t[g] if kind == "attn" else fv_t[:, TILES * g:TILES * g + TILES]
                for j in range(TILES):
                    for h in range(2):
                        d = HD * (2 * p + h) if (kind, p) != ("ffn", 1) else 2 * HD
                        ins = nc.tensor.matmul(outp[n % 2][HD * h:HD * h + HD, 2 * TOK * j:2 * TOK * (j + 1)],
                                               val[:, j, d:d + HD], pt_t[:, n % 2, j, h].rearrange("p i t -> p (i t)"),
                                               start=True, stop=True)
                ins.then_inc(attended, 1)

            def values(g, j):
                pe.wait_ge(wv_lo_s, 2)
                for half in range(2):
                    b = take("v", (g, j, half))
                    im, cols = GI * g + 2 * j, slice(384 * half, 384 * half + 384)
                    features(b[:, 0:384], wv_hi[:, :, cols], wv_lo[:, cols],
                             lambda t, c, rows: t[0:rows, c, im:im + 2, :].rearrange("p i s -> p (i s)"),
                             tokens_first=True).then_inc(projected, 1)

            def project_out(g, m):
                pe.wait_ge(wo_lo_s, 1)
                b = take("out", (g, m))
                cols = slice(128 * m, 128 * m + 128)
                for p in range(PAIRS):
                    pe.wait_ge(o_lo_s, ENTRY_OF[("attn", g, p)] + 1)
                    for z, (w, o) in enumerate(((wo_hi, o_hi), (wo_hi, o_lo), (wo_lo, o_hi))):
                        ins = nc.tensor.matmul(b[:, 0:GT], w[:, p, cols], o[:, g, p],
                                               start=(p == 0 and z == 0), stop=(p == PAIRS - 1 and z == 2))
                ins.then_inc(projected, 1)

            def project_experts(g, m):
                pe.wait_ge(o_lo_s, ENTRY_OF[("ffn", g, 1)] + 1)
                b = take("out2", (g, m))
                cols = slice(F_PROJ + 128 * m, F_PROJ + 128 * m + 128)
                ops = [(ffn_hi[:, 0, cols], y_hi[:, g, 0]), (ffn_hi[:, 0, cols], y_lo[:, g, 0]),
                       (ffn_lo[:, cols], y_hi[:, g, 0]), (ffn_hi[:, 1, cols], y_hi[:, g, 1]),
                       (ffn_hi[0:64, 1, cols], y_lo[0:64, g, 1])]
                for z, (w, y) in enumerate(ops):
                    ins = nc.tensor.matmul(b[:, 0:GT], w, y, start=(z == 0), stop=(z == 4))
                ins.then_inc(projected, 1)

            def statistic(kind, g):
                n = n_of[(kind, g)]
                if kind.startswith("mean"):
                    pe.wait_ge(res_s, 2 * n + 2)
                    src = r_t
                else:
                    pe.wait_ge(sq_s, n + 1)
                    src = sq_t
                b = take(kind, g)
                nc.tensor.matmul(b[:, 0:GT], mean_w, src[:, 0], start=True, stop=False)
                nc.tensor.matmul(b[:, 0:GT], mean_w[0:64], src[0:64, 1], start=False, stop=True
                                 ).then_inc(projected, 1)

            def gate_hidden(g):
                pe.wait_ge(h1_lo_s, NCH * g + NCH)
                pe.wait_ge(ffn_lo_s, 2)
                b = take("g1", g)
                cols = slice(F_GATE, F_GATE + 128)
                features(by_image(b[:, 0:GT]), ffn_hi[:, :, cols], ffn_lo[:, cols],
                         lambda t, c, rows: hcols(t, g, c, rows)).then_inc(projected, 1)

            def logits(g):
                b = take("lg", g)
                pe.wait_ge(ld_small, 16 * 3)
                pe.wait_ge(g1_s, 2 * g + 2)
                for im in range(GI):
                    ins = nc.tensor.matmul(b[:, 3 * im:3 * im + 3], g1_t[:, im].rearrange("p d s -> p (d s)"),
                                           fg2_w[:], start=True, stop=True)
                ins.then_inc(projected, 1)

            def expert_values(g, z):
                pe.wait_ge(h1_lo_s, NCH * g + NCH)
                pe.wait_ge(ffn_lo_s, 2)
                b = take("fv", (g, z))
                cols = slice(F_VAL, F_VAL + DIM)
                for jj in range(2):
                    im = GI * g + 4 * z + 2 * jj
                    ins = features(b[:, DIM * jj:DIM * jj + DIM], ffn_hi[:, :, cols], ffn_lo[:, cols],
                                   lambda t, c, rows: t[0:rows, c, im:im + 2, :].rearrange("p i s -> p (i s)"),
                                   tokens_first=True)
                ins.then_inc(projected, 1)

            for kind, *a in STEPS:
                if kind == "qk":
                    project_qk(*a)
                elif kind == "warm":
                    warm(a[0], WARM)
                elif kind == "s":
                    scores(*a)
                elif kind == "t":
                    transposes(*a)
                elif kind == "pv":
                    outputs(*a)
                elif kind == "v":
                    values(*a)
                elif kind == "out":
                    project_out(*a)
                elif kind == "out2":
                    project_experts(*a)
                elif kind in ("mean", "mean2", "var", "var2"):
                    statistic(kind, *a)
                elif kind == "gate":
                    gate_hidden(*a)
                elif kind == "lg":
                    logits(*a)
                elif kind == "fv":
                    expert_values(*a)


def kernel(**inputs):
    import ml_dtypes
    import numpy as np
    import concourse.bacc as bacc
    from concourse.bass_utils import run_bass_kernel_spmd

    f = {k: np.asarray(v) for k, v in inputs.items()}
    twice = lambda w: np.concatenate([w, w[..., 128:DIM]], axis=-1)
    chunks = lambda w: np.stack([w[0:128], np.concatenate([w[128:DIM]] * 2)], axis=1)
    x = f["x"].reshape(GROUPS, GI, 3, 6, 16, 6, 16).transpose(2, 4, 6, 0, 1, 3, 5)
    x = x.reshape(PK, 128, GROUPS, GT).transpose(1, 2, 0, 3)
    qkv = f["L0_attn_w_qkv"].reshape(DIM, PAIRS, 2, 3, HD)
    w_qk = chunks(qkv[:, :, :, 0:2].transpose(0, 1, 3, 2, 4).reshape(DIM, PAIRS, 256)).transpose(0, 2, 1, 3)

    wqk, bqk = f["L0_ffn_Wqk"].reshape(DIM, 2, 3, HD), f["L0_ffn_bqk"].reshape(2, 3, HD)
    order = [(0, 0), (0, 1), (1, 0), (1, 1), (0, 2), (0, 2), (1, 2), (1, 2)]
    f_w = np.concatenate([wqk[:, a, e] for a, e in order] + [f["L0_ffn_Wg1"], np.zeros((DIM, 96), np.float32)]
                         + list(f["L0_ffn_Wv"]) + [twice(f["L0_ffn_Wp"])], axis=1)

    biases = np.zeros((128, B_END), np.float32)
    for col, name in ((B_TOK, "L0_tok_bp"), (B_OUT, "L0_attn_b_out"), (B_FFN, "L0_ffn_bp")):
        biases[:, col:col + NCH] = twice(f[name]).reshape(NCH, 128).T
    for n in range(4):
        biases[:, B_QK + n] = np.concatenate([bqk[order[2 * n]], bqk[order[2 * n + 1]]])
    biases[0:HD, B_CONVW:B_CONVW + 3] = f["L0_ffn_conv_w"].reshape(HD, 3)
    biases[0:HD, B_CONVB] = f["L0_ffn_conv_b"]
    biases[0:32, B_G1] = f["L0_ffn_bg1"]
    pos_bias = np.zeros((128, TOK), np.float32)
    pos_bias[0:TOK] = pos_bias[64:64 + TOK] = f["L0_ffn_pos_bias"][0:TOK, 0:TOK]

    tok = np.arange(TOK)
    dist = tok[None, :] - tok[:, None]
    band, causal, outside = np.zeros((128, TOK)), np.zeros((128, TOK)), np.ones(128)
    for lo in (0, 64):
        band[lo:lo + TOK] = np.where(abs(dist) <= WINDOW_SIDE, 0.0, NEG)
        causal[lo:lo + TOK] = np.where(dist > 0, NEG, 0.0)
        outside[lo:lo + TOK] = 2 * WINDOW_SIDE + 1 - (abs(dist) <= WINDOW_SIDE).sum(1)
    consts = np.zeros((128, C_END), np.float32)
    consts[:, C_IDENT:C_IDENT + 128] = np.eye(128)
    consts[:, C_CAUSAL:C_CAUSAL + TOK] = causal
    consts[:, C_OUTSIDE] = outside
    consts[:, C_EPS] = 1e-5
    consts[:, C_MEAN:C_MEAN + 128] = 1.0 / DIM
    bf_consts = np.concatenate([np.eye(128), band, causal], axis=1).astype(ml_dtypes.bfloat16)

    arrays = {
        "x_t": x,
        "tok_w": twice(f["L0_tok_Wp"].T).reshape(PK, 128, DUP).transpose(1, 0, 2),
        "w_qk": w_qk,
        "w_v": chunks(qkv[:, :, :, 2].reshape(DIM, PATCH)),
        "w_out": twice(f["L0_attn_w_out"]).reshape(PAIRS, 128, DUP).transpose(1, 0, 2),
        "f_w": chunks(f_w),
        "f_g2": np.concatenate([f["L0_ffn_Wg2"], f["L0_ffn_bg2"][None]]),
        "f_bv": np.stack([f["L0_ffn_bv"].reshape(DIM)] * 128),
        "pos_bias": pos_bias, "biases": biases, "consts": consts, "bf_consts": bf_consts,
    }
    arrays = {k: np.ascontiguousarray(a) for k, a in arrays.items()}
    nc = bacc.Bacc("TRN2", target_bir_lowering=False, num_devices=1)
    args = [nc.dram_tensor(k, a.shape, mybir.dt.from_np(a.dtype), kind="ExternalInput").ap() for k, a in arrays.items()]
    out = nc.dram_tensor("out_t", (DIM, IMAGES * TOK), F32, kind="ExternalOutput").ap()
    vit_tower(nc, *args, out)
    got = run_bass_kernel_spmd(nc, [arrays], core_ids=[0]).results[0]["out_t"]
    return np.ascontiguousarray(got.T.reshape(IMAGES, TOK, DIM))
```
